# Optimizing a Trainium2 kernel written in Bass

```python
import numpy as np
import jax
import jax.numpy as jnp

def _softmax(x, axis=-1):
    return jax.nn.softmax(x, axis=axis)

def _gelu(x):
    return jax.nn.gelu(x, approximate=True)

def _silu(x):
    return jax.nn.silu(x)

def _sigmoid(x):
    return jax.nn.sigmoid(x)

def _layernorm(x, axis=-1, eps=1e-05):
    m = jnp.mean(x, axis=axis, keepdims=True)
    v = jnp.var(x, axis=axis, keepdims=True)
    return (x - m) / jnp.sqrt(v + eps)

def _scatter_add(tgt, idx, src, axis=0):
    return tgt.at[idx].add(src)

def _segment_sum(src, seg, n):
    return jax.ops.segment_sum(src, seg, n)
kernel_name = 'mk_seq_preln_d1_jaxref_r4_d5aabf'

def setup_inputs(seed: int=0):
    np.random.seed(seed)
    _w = jnp.asarray

    def _L0_attn_setup():
        import jax, jax.numpy as jnp
        import numpy as np
        DIM = 256
        NUM_HEADS = 16
        HEAD_DIM = DIM // NUM_HEADS
        WINDOW = 64
        B, L = (2, 512)
        EPS = 1e-05
        INIT_STD = 0.01

        def rmsnorm(x, w):
            x = jnp.clip(x, -10000.0, 10000.0)
            rms = jnp.sqrt(jnp.maximum(jnp.mean(x * x, axis=-1, keepdims=True), EPS) + EPS)
            out = x / rms * w
            return jnp.where(jnp.isfinite(out), out, jnp.zeros_like(out))
        key = jax.random.key(seed)
        ks = jax.random.split(key, 6)
        return {'x': jax.random.normal(ks[0], (B, L, DIM), dtype=jnp.float32), 'wq_w': jax.random.normal(ks[1], (DIM, DIM), dtype=jnp.float32) * INIT_STD, 'wq_b': jnp.zeros((DIM,), jnp.float32), 'wk_w': jax.random.normal(ks[2], (DIM, DIM), dtype=jnp.float32) * INIT_STD, 'wk_b': jnp.zeros((DIM,), jnp.float32), 'wv_w': jax.random.normal(ks[3], (DIM, DIM), dtype=jnp.float32) * INIT_STD, 'wv_b': jnp.zeros((DIM,), jnp.float32), 'wo_w': jax.random.normal(ks[4], (DIM, DIM), dtype=jnp.float32) * INIT_STD, 'wo_b': jnp.zeros((DIM,), jnp.float32), 'qn_w': jnp.ones((HEAD_DIM,), jnp.float32), 'kn_w': jnp.ones((HEAD_DIM,), jnp.float32)}
    _L0_attn_in = _L0_attn_setup()

    def _L0_ffn_setup():
        import jax, jax.numpy as jnp
        import numpy as np
        DIM = 256

        def _reference_tuple_inner(x, W_r, W_k, W_v, mu_r, mu_k):
            B, T, C = x.shape
            x_prev = jnp.concatenate([jnp.zeros((B, 1, C), x.dtype), x[:, :-1, :]], axis=1)
            xr = mu_r * x + (1.0 - mu_r) * x_prev
            xk = mu_k * x + (1.0 - mu_k) * x_prev
            r = jax.nn.sigmoid(jnp.einsum('btc,dc->btd', xr, W_r))
            k = jnp.einsum('btc,dc->btd', xk, W_k)
            k_act = jnp.square(jax.nn.relu(k))
            out = r * jnp.einsum('btc,dc->btd', k_act, W_v)
            new_state = x[:, -1, :]
            return (out, new_state)
        key = jax.random.key(seed)
        ks = jax.random.split(key, 6)
        B, T, C = (8, 512, DIM)
        x = jax.random.normal(ks[0], (B, T, C), dtype=jnp.float32)
        s = 1.0 / np.sqrt(C)
        W_r = jax.random.uniform(ks[1], (C, C), jnp.float32, -s, s)
        W_k = jax.random.uniform(ks[2], (C, C), jnp.float32, -s, s)
        W_v = jax.random.uniform(ks[3], (C, C), jnp.float32, -s, s)
        mu_r = jax.random.uniform(ks[4], (C,), jnp.float32)
        mu_k = jax.random.uniform(ks[5], (C,), jnp.float32)
        return {'x': x, 'W_r': W_r, 'W_k': W_k, 'W_v': W_v, 'mu_r': mu_r, 'mu_k': mu_k}
    _L0_ffn_in = _L0_ffn_setup()
    _d = {'L0_attn_x': _L0_attn_in['x'], 'L0_attn_wq_w': _L0_attn_in['wq_w'], 'L0_attn_wq_b': _L0_attn_in['wq_b'], 'L0_attn_wk_w': _L0_attn_in['wk_w'], 'L0_attn_wk_b': _L0_attn_in['wk_b'], 'L0_attn_wv_w': _L0_attn_in['wv_w'], 'L0_attn_wv_b': _L0_attn_in['wv_b'], 'L0_attn_wo_w': _L0_attn_in['wo_w'], 'L0_attn_wo_b': _L0_attn_in['wo_b'], 'L0_attn_qn_w': _L0_attn_in['qn_w'], 'L0_attn_kn_w': _L0_attn_in['kn_w'], 'L0_ffn_W_r': _L0_ffn_in['W_r'], 'L0_ffn_W_k': _L0_ffn_in['W_k'], 'L0_ffn_W_v': _L0_ffn_in['W_v'], 'L0_ffn_mu_r': _L0_ffn_in['mu_r'], 'L0_ffn_mu_k': _L0_ffn_in['mu_k']}
    _x0 = _d['L0_attn_x']
    _d['L0_attn_x'] = jax.random.normal(jax.random.fold_in(jax.random.key(seed), 1), (32, 512, 256), dtype=_x0.dtype)
    del _x0
    return _d

def reference(L0_attn_x, L0_attn_wq_w, L0_attn_wq_b, L0_attn_wk_w, L0_attn_wk_b, L0_attn_wv_w, L0_attn_wv_b, L0_attn_wo_w, L0_attn_wo_b, L0_attn_qn_w, L0_attn_kn_w, L0_ffn_W_r, L0_ffn_W_k, L0_ffn_W_v, L0_ffn_mu_r, L0_ffn_mu_k):

    def _L0_attn_ref(x, wq_w, wq_b, wk_w, wk_b, wv_w, wv_b, wo_w, wo_b, qn_w, kn_w):
        import jax, jax.numpy as jnp
        import numpy as np
        DIM = 256
        NUM_HEADS = 16
        HEAD_DIM = DIM // NUM_HEADS
        WINDOW = 64
        B, L = (2, 512)
        EPS = 1e-05
        INIT_STD = 0.01

        def rmsnorm(x, w):
            x = jnp.clip(x, -10000.0, 10000.0)
            rms = jnp.sqrt(jnp.maximum(jnp.mean(x * x, axis=-1, keepdims=True), EPS) + EPS)
            out = x / rms * w
            return jnp.where(jnp.isfinite(out), out, jnp.zeros_like(out))
        b, l, d = x.shape
        x = x.astype(jnp.float32)

        def proj(w, bias):
            return (x @ w.T + bias).reshape(b, l, NUM_HEADS, HEAD_DIM).transpose(0, 2, 1, 3)
        q = rmsnorm(proj(wq_w, wq_b), qn_w)
        k = rmsnorm(proj(wk_w, wk_b), kn_w)
        v = proj(wv_w, wv_b)
        scale = HEAD_DIM ** (-0.5)
        i = jnp.arange(l)
        allowed = (i[None, :] <= i[:, None]) & (i[:, None] - i[None, :] < WINDOW)
        scores = jnp.einsum('bhqd,bhkd->bhqk', q, k) * scale
        scores = jnp.where(allowed[None, None], scores, -jnp.inf)
        attn = jax.nn.softmax(scores, axis=-1)
        out = jnp.einsum('bhqk,bhkd->bhqd', attn, v)
        out = jnp.where(jnp.isfinite(out), out, jnp.zeros_like(out))
        out = out.transpose(0, 2, 1, 3).reshape(b, l, d)
        return out @ wo_w.T + wo_b

    def _L0_ffn_ref(x, W_r, W_k, W_v, mu_r, mu_k):
        import jax, jax.numpy as jnp
        import numpy as np
        DIM = 256

        def _reference_tuple_inner(x, W_r, W_k, W_v, mu_r, mu_k):
            B, T, C = x.shape
            x_prev = jnp.concatenate([jnp.zeros((B, 1, C), x.dtype), x[:, :-1, :]], axis=1)
            xr = mu_r * x + (1.0 - mu_r) * x_prev
            xk = mu_k * x + (1.0 - mu_k) * x_prev
            r = jax.nn.sigmoid(jnp.einsum('btc,dc->btd', xr, W_r))
            k = jnp.einsum('btc,dc->btd', xk, W_k)
            k_act = jnp.square(jax.nn.relu(k))
            out = r * jnp.einsum('btc,dc->btd', k_act, W_v)
            new_state = x[:, -1, :]
            return (out, new_state)
        return _reference_tuple_inner(x, W_r, W_k, W_v, mu_r, mu_k)[0]
    x = L0_attn_x
    x = x + _L0_attn_ref(_layernorm(x, axis=-1), L0_attn_wq_w, L0_attn_wq_b, L0_attn_wk_w, L0_attn_wk_b, L0_attn_wv_w, L0_attn_wv_b, L0_attn_wo_w, L0_attn_wo_b, L0_attn_qn_w, L0_attn_kn_w)
    x = x + _L0_ffn_ref(_layernorm(x, axis=-1), L0_ffn_W_r, L0_ffn_W_k, L0_ffn_W_v, L0_ffn_mu_r, L0_ffn_mu_k)
    return x

_drawn_inputs = setup_inputs


def setup_inputs(seed=0):
    import zlib

    import numpy as np

    out = dict(_drawn_inputs(seed))
    spreads = {'L0_attn_wq_b': (0.0, 0.8),
     'L0_attn_wk_b': (0.0, 0.8),
     'L0_attn_wv_b': (0.0, 0.501),
     'L0_attn_wo_b': (0.0, 0.1),
     'L0_attn_qn_w': (1.0, 0.6),
     'L0_attn_kn_w': (1.0, 0.6)}
    factors = {'L0_attn_wq_w': 8.0,
     'L0_attn_wk_w': 8.0,
     'L0_attn_wv_w': 8.0,
     'L0_attn_wo_w': 3.217,
     'L0_ffn_W_r': 3.17,
     'L0_ffn_mu_r': 6.428}
    for name, (base, spread) in spreads.items():
        noise = np.random.default_rng([zlib.crc32(name.encode()), seed]).standard_normal(out[name].shape)
        drawn = base * np.exp(spread * noise) if base else spread * noise
        out[name] = jnp.asarray(drawn.astype(out[name].dtype))
    for name, factor in factors.items():
        out[name] = (out[name] * factor).astype(out[name].dtype)
    return out
```

```python
from contextlib import ExitStack

import numpy as np
import concourse.bass as bass
from concourse import mybir

FP32 = mybir.dt.float32
BF16 = mybir.dt.bfloat16
ALU = mybir.AluOpType
ACT = mybir.ActivationFunctionType
AX = mybir.AxisListType

SEQS, L, D = 32, 512, 256
HEADS, HD = 16, 16
WINDOW = 64
P = 128
TILES = L // P
KT = D // P
BLOCKS = L // WINDOW
PARTS = 3
Q_SLOTS = (0, 0, 0, 1, 1, 2)
K_SLOTS = (0, 1, 2, 0, 1, 0)
STACK = HD * len(Q_SLOTS)
ROWS = STACK + PARTS
LN_EPS = 1e-5
RMS_EPS = 1e-5
CLIP = 1e4
SCALE = float(HD) ** -0.5
MASKED = -1e30
QUADS = HEADS // 4


class Seq:

    def __init__(self, pair, offset):
        self.pair, self.offset = pair, offset
        self.n = 2 * pair + offset
        self.parity = offset % 2
        self.half = pair + offset // 2

    def shifted(self, by):
        return Seq(self.pair, self.offset + by)

    def after(self, per, k):
        return self.n * per + k

    def after_half(self, per, k):
        return self.half * per + k


def past(count):
    return not isinstance(count, int) or count > 0


def held(eng, count):
    return count if isinstance(count, int) else eng.to_reg(count)


def build(nc, x, wqkT, wvT, woP, wrT, wkT, wfT, bqkv, bo, qn, kn, mu, out):
    ctx = ExitStack()
    with ctx:
        def sb(name, shape, dt=FP32):
            return ctx.enter_context(nc.sbuf_tensor(name, shape, dt))

        def ps(name):
            return ctx.enter_context(nc.psum_tensor(name, [P, 512], FP32))

        def sem(name):
            return ctx.enter_context(nc.semaphore(name))

        w_qk = sb("w_qk", [P, KT, 2 * D])
        w_v = sb("w_v", [P, KT, D])
        w_o = sb("w_o", [P, QUADS, D])
        w_r = sb("w_r", [P, KT, D])
        w_k = sb("w_k", [P, KT, D])
        w_f = sb("w_f", [P, KT, D])
        bias_p = sb("bias_p", [65, 4 * D], BF16)
        ones_rows = sb("ones_rows", [65, P], BF16)
        qn_col = sb("qn_col", [P, 1])
        kn_col = sb("kn_col", [P, 1])
        qk_scale = sb("qk_scale", [P, 1])
        mu_col = sb("mu_col", [P, 2, KT])
        one_minus_mu = sb("one_minus_mu", [P, 2, KT])
        minus_half = sb("minus_half", [P, 2 * HEADS * TILES])
        ident = sb("ident", [P, P])
        ident_b = sb("ident_b", [P, P], BF16)
        mask_a = [sb(f"mask_a{i}", [P, 4, P], BF16) for i in range(2)]
        mask_b = [sb(f"mask_b{i}", [P, 8, WINDOW], BF16) for i in range(2)]

        x_in = [sb(f"x_in{i}", [P, TILES, D]) for i in range(2)]
        xn = sb("xn", [P, TILES, D])
        xT = sb("xT", [P, KT, L])
        qk = sb("qk", [P, TILES, 2 * D])
        bias = qk[0:1, 0:2, :].rearrange("p a n -> p (a n)")
        bias_rest = qk[0:1, 2:4, :].rearrange("p a n -> p (a n)")
        sq = [sb(f"sq{i}", [P, 2 * D]) for i in range(2)]
        rms = sb("rms", [P, TILES, 2 * HEADS])
        parts = sb("parts", [P, 4, PARTS, L], BF16)
        rest = [sb(f"rest{i}", [P, 4, P]) for i in range(2)]
        q_st = [sb(f"q_st{i}", [P, HEADS, L], BF16) for i in range(2)]
        k_st = [sb(f"k_st{i}", [P, HEADS, L], BF16) for i in range(2)]
        v_own = [sb(f"v_own{i}", [P, TILES, HEADS, HD + 1]) for i in range(2)]
        v_mix = [sb(f"v_mix{i}", [P, TILES, HEADS, HD + 1]) for i in range(2)]
        smax = sb("smax", [P, TILES, HEADS])
        neg_rest = sb("neg_rest", [HEADS, L])
        neg_p = [sb(f"neg_p{i}", [HEADS, L], BF16) for i in range(PARTS)]
        prob = [sb(f"prob{i}", [P, 8, WINDOW]) for i in range(3)]
        o_tok = sb("o_tok", [P, 16, 32])
        o_inv = sb("o_inv", [P, 16])
        o_nrm = sb("o_nrm", [P, 16, 32])
        oT = sb("oT", [P, TILES, QUADS, P])
        x1 = sb("x1", [P, TILES, D])
        x2T = sb("x2T", [P, KT, L + 1])
        mixa = [sb(f"mixa{i}", [P, L]) for i in range(2)]
        xr = sb("xr", [P, KT, L])
        xk = sb("xk", [P, KT, L])
        kact = sb("kact", [P, KT, L])
        gate = sb("gate", [P, TILES, D])
        y = sb("y", [P, TILES, D])
        st1 = sb("st1", [P, TILES, 6])
        mv1 = sb("mv1", [P, TILES, 2])
        rstd1 = sb("rstd1", [P, TILES])
        st2 = sb("st2", [P, TILES, 6])
        mv2 = sb("mv2", [P, TILES, 2])
        rstd2 = sb("rstd2", [P, TILES])

        bank_t = [ps(f"bank_t{i}") for i in range(2)]
        bank_p = [ps(f"bank_p{i}") for i in range(2)]
        bank_s = [ps(f"bank_s{i}") for i in range(2)]
        bank_o = [ps(f"bank_o{i}") for i in range(2)]

        scratch = [nc.dram_tensor(f"scratch{i}", (2, D, PARTS, L), BF16).ap() for i in range(2)]

        consts_loaded = sem("consts_loaded")
        pool_consts = sem("pool_consts")
        pool_step = sem("pool_step")
        dve_consts = sem("dve_consts")
        x_loaded = [sem(f"x_loaded{i}") for i in range(2)]
        y_stored = sem("y_stored")
        scratch_written = sem("scratch_written")
        stack_loaded = [sem(f"stack_loaded{i}") for i in range(2)]
        max_rows_loaded = sem("max_rows_loaded")
        ln1_stats, ln1_mv, xn1_ready = sem("ln1_stats"), sem("ln1_mv"), sem("xn1_ready")
        ln2_stats, ln2_mv, xn2_ready = sem("ln2_stats"), sem("ln2_mv"), sem("xn2_ready")
        qk_clipped, sumsq_ready, qkn_ready = sem("qk_clipped"), sem("sumsq_ready"), sem("qkn_ready")
        rest_ready, max_ready, neg_rest_ready = sem("rest_ready"), sem("max_ready"), sem("neg_rest_ready")
        mixed, kvr_ready, y_ready = sem("mixed"), sem("kvr_ready"), sem("y_ready")
        o_turned, o_inverse, o_normed, oT_ready = sem("o_turned"), sem("o_inverse"), sem("o_normed"), sem("oT_ready")
        x1_ready = sem("x1_ready")
        ln1_eps, ln1_rstd, ln2_eps, ln2_rstd = sem("ln1_eps"), sem("ln1_rstd"), sem("ln2_eps"), sem("ln2_rstd")
        rms_mean, rms_eps, rms_ready = sem("rms_mean"), sem("rms_eps"), sem("rms_ready")
        part2_ready, neg2_ready = sem("part2_ready"), sem("neg2_ready")
        xT_ready, sq_ready, v_ready = sem("xT_ready"), sem("sq_ready"), sem("v_ready")
        part0_ready, part1_ready = sem("part0_ready"), sem("part1_ready")
        neg0_ready, neg1_ready = sem("neg0_ready"), sem("neg1_ready")
        x2T_ready, mixa_ready, relu_ready, kact_ready, gate_ready = (
            sem("x2T_ready"), sem("mixa_ready"), sem("relu_ready"), sem("kact_ready"), sem("gate_ready"))
        prob_ready = sem("prob_ready")
        xT_done, qk_done, v_done, qkT_done = sem("xT_done"), sem("qk_done"), sem("v_done"), sem("qkT_done")
        a_done, maxT_done, b_done, pv_done, wo_done = (
            sem("a_done"), sem("maxT_done"), sem("b_done"), sem("pv_done"), sem("wo_done"))
        x2T_done, k_done, r_done, kv_done = sem("x2T_done"), sem("k_done"), sem("r_done"), sem("kv_done")

        CONSTS = 11
        BANKS = TILES * HEADS // 4

        def schedule(eng, body):
            body(Seq(0, -1), False, True, False)
            body(Seq(0, 0), True, True, False)
            body(Seq(0, 1), True, True, True)
            with eng.Fori(0, (SEQS - 4) // 2) as pair:
                body(Seq(pair, 2), True, True, True)
                body(Seq(pair, 3), True, True, True)
            body(Seq(0, SEQS - 2), True, True, True)
            body(Seq(0, SEQS - 1), True, False, True)
            body(Seq(0, SEQS), False, False, True)

        block = ctx.enter_context(nc.Block())

        @block.sync
        def _(sp):
            for dst, src in ((w_qk, wqkT), (w_v, wvT), (w_r, wrT), (w_k, wkT), (w_f, wfT)):
                sp.dma_start(dst[:, :, :], src.rearrange("(k p) n -> p k n", p=P)).then_inc(consts_loaded, 16)
            sp.dma_start(w_o[:, :, :], woP.rearrange("(k p) n -> p k n", p=P)).then_inc(consts_loaded, 16)
            sp.dma_start(bias[:, 0:3 * D], bqkv).then_inc(consts_loaded, 16)
            sp.dma_start(bias[:, 3 * D:4 * D], bo).then_inc(consts_loaded, 16)
            sp.dma_start(qn_col[:, :], qn).then_inc(consts_loaded, 16)
            sp.dma_start(kn_col[:, :], kn).then_inc(consts_loaded, 16)
            sp.dma_start(mu_col[:, :, :], mu).then_inc(consts_loaded, 16)

            def load_x(s):
                sp.dma_start(x_in[s.parity][:, :, :], x[bass.ds(s.n * L, L), :].rearrange("(t p) d -> p t d", p=P))\
                    .then_inc(x_loaded[s.parity], 16)

            def body(s, attend, front, ffn):
                f, g = s.shifted(1), s.shifted(-1)
                if not attend and front:
                    load_x(f)
                    load_x(s.shifted(2))
                if attend:
                    sp.wait_ge(neg0_ready, s.after(1, 1))
                    sp.wait_ge(neg1_ready, s.after(1, 1))
                    sp.wait_ge(neg2_ready, s.after(1, 1))
                    for i in range(PARTS):
                        sp.dma_start(q_st[s.parity][STACK + i:STACK + i + 1, :, :], neg_p[i][:, :])\
                            .then_inc(max_rows_loaded, 16)
                if front:
                    sp.wait_ge(part0_ready, f.after(TILES, TILES))
                    sp.wait_ge(part1_ready, f.after(TILES, TILES))
                    sp.wait_ge(part2_ready, f.after(TILES, TILES))
                    sp.dma_start(scratch[f.parity].rearrange("w (g p) a t -> p (w g) (a t)", p=P),
                                 parts[:, :, :, :].rearrange("p b a t -> p b (a t)")).then_inc(scratch_written, 16)
                    if past(count := f.after(BANKS, -BANKS)):
                        count = held(sp, count)
                        sp.wait_ge(consts_loaded, 16 * CONSTS)
                        sp.wait_ge(b_done, count)
                    if past(count := f.after(16, 16)):
                        count = held(sp, count)
                        sp.wait_ge(consts_loaded, 16 * CONSTS)
                        sp.wait_ge(scratch_written, count)
                    for st, which, slots in ((q_st, 0, Q_SLOTS), (k_st, 1, K_SLOTS)):
                        for slot, part in enumerate(slots):
                            src = scratch[f.parity][which, :, part, :].rearrange("(h r) t -> r h t", r=HD)
                            sp.dma_start(st[f.parity][HD * slot:HD * slot + HD, :, :], src).then_inc(stack_loaded[f.parity], 16)
                if ffn:
                    if past(count := g.after(TILES, TILES)):
                        count = held(sp, count)
                        sp.wait_ge(consts_loaded, 16 * CONSTS)
                        sp.wait_ge(y_ready, count)
                    sp.dma_start(out[bass.ds(g.n * L, L), :].rearrange("(t p) d -> p t d", p=P), y[:, :, :])\
                        .then_inc(y_stored, 16)
                if attend and front and not (isinstance(s.n, int) and s.n + 2 >= SEQS):
                    if past(count := s.after(TILES, TILES)):
                        count = held(sp, count)
                        sp.wait_ge(consts_loaded, 16 * CONSTS)
                        sp.wait_ge(x1_ready, count)
                    load_x(s.shifted(2))

            schedule(sp, body)
            sp.wait_ge(y_stored, 16 * SEQS)

        @block.gpsimd
        def _(pool):
            steps = [0]

            def const(instruction):
                steps[0] += 1
                instruction.then_inc(pool_step, 1)
                pool.wait_ge(pool_step, steps[0])

            def fill_mask(m, rows, pattern, base, per_row):
                view = m[rows[0]:rows[1], :, :]
                const(nc.gpsimd.affine_select(out=view, in_=view, compare_op=ALU.is_ge, fill=MASKED,
                                              base=base, pattern=pattern, channel_multiplier=per_row))

            for m in (ident, ident_b):
                const(nc.gpsimd.memset(m[:, :], 0.0))
                const(nc.gpsimd.affine_select(out=m[:, :], in_=m[:, :], compare_op=ALU.not_equal, fill=1.0,
                                              base=0, pattern=[[-1, P]], channel_multiplier=1))
            for m in (*mask_a, *mask_b):
                const(nc.gpsimd.memset(m[:, :, :], 0.0))
            W = WINDOW
            for i, m in enumerate(mask_a):
                for half in range(2):
                    rows = (W * half, W * half + W)
                    fill_mask(m, rows, [[0, 4], [1, P]], -1, -1)
                    fill_mask(m, rows, [[0, 4], [-1, P]], W, 1)
                if i == 0:
                    fill_mask(m, (0, W), [[0, 4], [1, P]], -W, 0)
            for m in mask_b:
                fill_mask(m, (0, P), [[0, 8], [-1, W]], -1, 1)
                fill_mask(m, (0, P), [[0, 8], [1, W]], W, -1)
            fill_mask(mask_b[0], (0, W), [[0, 8], [0, W]], -1, 0)
            const(nc.gpsimd.memset(minus_half[:, :], -0.5))
            nc.gpsimd.memset(ones_rows[:, :], 1.0).then_inc(pool_consts, 1)

            def inverse_root(v, eps_sem, eps_count, done):
                pool.wait_ge(eps_sem, eps_count)
                n = v.shape[1]
                nc.gpsimd.tensor_tensor(v, v, minus_half[:, 0:n], ALU.pow).then_inc(done, 1)

            def body(s, attend, front, ffn):
                f, g = s.shifted(1), s.shifted(-1)
                if ffn:
                    if past(count := g.after(TILES, TILES)):
                        count = held(pool, count)
                        pool.wait_ge(dve_consts, 1)
                        pool.wait_ge(ln2_mv, count)
                    nc.gpsimd.tensor_scalar(rstd2[:, :], mv2[:, :, 1], LN_EPS, None, ALU.add).then_inc(ln2_eps, 1)
                    inverse_root(rstd2[:, :], ln2_eps, g.after(1, 1), ln2_rstd)
                if front:
                    if past(count := f.after(TILES, TILES)):
                        count = held(pool, count)
                        pool.wait_ge(dve_consts, 1)
                        pool.wait_ge(ln1_mv, count)
                    nc.gpsimd.tensor_scalar(rstd1[:, :], mv1[:, :, 1], LN_EPS, None, ALU.add).then_inc(ln1_eps, 1)
                    inverse_root(rstd1[:, :], ln1_eps, f.after(1, 1), ln1_rstd)
                    flat = rms[:, :, :].rearrange("p t h -> p (t h)")
                    if past(count := f.after(TILES, TILES)):
                        count = held(pool, count)
                        pool.wait_ge(dve_consts, 1)
                        pool.wait_ge(sumsq_ready, count)
                    nc.gpsimd.tensor_scalar(flat, flat, 1.0 / HD, RMS_EPS, ALU.mult, ALU.max).then_inc(rms_mean, 1)
                    if past(count := f.after(1, 1)):
                        count = held(pool, count)
                        pool.wait_ge(dve_consts, 1)
                        pool.wait_ge(rms_mean, count)
                    nc.gpsimd.tensor_scalar(flat, flat, RMS_EPS, None, ALU.add).then_inc(rms_eps, 1)
                    inverse_root(flat, rms_eps, f.after(1, 1), rms_ready)
                if attend:
                    pool.wait_ge(neg_rest_ready, s.after(1, 1))
                    pool.wait_ge(neg1_ready, s.after(1, 1))
                    if past(count := s.after(16 * PARTS, 0)):
                        pool.wait_ge(max_rows_loaded, count)
                    nc.gpsimd.tensor_tensor(neg_p[2][:, :], neg_rest[:, :], neg_p[1][:, :], ALU.subtract)\
                        .then_inc(neg2_ready, 1)
                if front:
                    for t in range(TILES):
                        if t == 0:
                            if past(count := f.after(16, 0)):
                                pool.wait_ge(scratch_written, count)
                        pool.wait_ge(rest_ready, f.after(TILES, t + 1))
                        pool.wait_ge(part1_ready, f.after(TILES, t + 1))
                        nc.gpsimd.tensor_tensor(parts[:, :, 2, P * t:P * t + P], rest[t % 2][:, :, :],
                                                parts[:, :, 1, P * t:P * t + P], ALU.subtract)\
                            .then_inc(part2_ready, 1)

            schedule(pool, body)

        @block.scalar
        def _(act):
            def body(s, attend, front, ffn):
                f, g = s.shifted(1), s.shifted(-1)
                if ffn:
                    for k in range(KT):
                        act.wait_ge(x2T_done, g.after(KT, k + 1))
                        if k == 0:
                            if past(count := g.after(2 * KT, 0)):
                                act.wait_ge(mixed, count)
                        nc.scalar.activation(x2T[:, k, 1:L + 1], bank_t[k][:, :], ACT.Copy).then_inc(x2T_ready, 1)
                if front:
                    for k in range(KT):
                        act.wait_ge(xT_done, f.after(KT, k + 1))
                        if k == 0:
                            if past(count := f.after(TILES, 0)):
                                act.wait_ge(v_done, count)
                        nc.scalar.activation(xT[:, k, :], bank_t[k][:, :], ACT.Copy).then_inc(xT_ready, 1)
                    for t in range(TILES):
                        act.wait_ge(v_done, f.after(TILES, t + 1))
                        if t == 0:
                            if past(count := f.after(BANKS, -BANKS)):
                                act.wait_ge(pv_done, count)
                        v4 = bank_p[1][:, 0:D].rearrange("p (h d) -> p h d", d=HD)
                        u = f.parity
                        nc.scalar.activation(v_own[u][:, t, :, 0:HD], v4, ACT.Copy)
                        last = nc.scalar.activation(v_mix[u][WINDOW:P, t, :, 0:HD], v4[0:WINDOW], ACT.Copy)
                        if t + 1 < TILES:
                            last = nc.scalar.activation(v_mix[u][0:WINDOW, t + 1, :, 0:HD], v4[WINDOW:P], ACT.Copy)
                        last.then_inc(v_ready, 1)
                        act.wait_ge(qk_clipped, f.after(TILES, t + 1))
                        if past(count := f.after(TILES, t - 1)):
                            act.wait_ge(sumsq_ready, count)
                        nc.scalar.activation(sq[t % 2][:, :], qk[:, t, :], ACT.Square).then_inc(sq_ready, 1)
                if attend:
                    act.wait_ge(maxT_done, s.after(1, 1))
                    if past(count := s.after(16 * PARTS, 0)):
                        act.wait_ge(max_rows_loaded, count)
                    nc.scalar.activation(neg_p[0][:, :], bank_t[0][0:HEADS, :], ACT.Copy, scale=-1.0)\
                        .then_inc(neg0_ready, 1)
                    act.wait_ge(neg_rest_ready, s.after(1, 1))
                    nc.scalar.activation(neg_p[1][:, :], neg_rest[:, :], ACT.Copy).then_inc(neg1_ready, 1)
                if ffn:
                    for c in range(2 * KT):
                        which, k = c // KT, c % KT
                        act.wait_ge(x2T_ready, g.after(KT, KT))
                        if past(count := g.after(2 * KT, max(c - 1, 0))):
                            act.wait_ge(mixed, count)
                        nc.scalar.activation(mixa[c % 2][:, :], x2T[:, k, 0:L], ACT.Copy,
                                             scale=one_minus_mu[:, which, k:k + 1]).then_inc(mixa_ready, 1)
                    for m in range(KT):
                        act.wait_ge(k_done, g.after(KT, m + 1))
                        if m == 0:
                            if past(count := g.after(TILES, 0)):
                                act.wait_ge(kv_done, count)
                        nc.scalar.activation(kact[:, m, :], bank_t[m][:, :], ACT.Relu).then_inc(relu_ready, 1)
                        act.wait_ge(relu_ready, g.after(KT, m + 1))
                        nc.scalar.activation(kact[:, m, :], kact[:, m, :], ACT.Square).then_inc(kact_ready, 1)
                    for t in range(TILES):
                        act.wait_ge(r_done, g.after(TILES, t + 1))
                        if t == 0:
                            if past(count := g.after(TILES, 0)):
                                act.wait_ge(y_ready, count)
                        nc.scalar.activation(gate[:, t, :], bank_p[t % 2][:, 0:D], ACT.Tanh, scale=0.5)\
                            .then_inc(gate_ready, 1)
                if front:
                    for t in range(TILES):
                        act.wait_ge(qkT_done, f.after(TILES, t + 1))
                        if t == 0:
                            if past(count := f.after(16, 0)):
                                act.wait_ge(scratch_written, count)
                        b4 = bank_t[t % 2][:, :].rearrange("p (b n) -> p b n", b=4)
                        cols = slice(P * t, P * t + P)
                        nc.scalar.activation(parts[:, 0:2, 0, cols], b4[:, 0:2, :], ACT.Copy, scale=qk_scale[:, :])
                        nc.scalar.activation(parts[:, 2:4, 0, cols], b4[:, 2:4, :], ACT.Copy).then_inc(part0_ready, 1)
                        act.wait_ge(rest_ready, f.after(TILES, t + 1))
                        nc.scalar.activation(parts[:, :, 1, cols], rest[t % 2][:, :, :], ACT.Copy)\
                            .then_inc(part1_ready, 1)
                if attend:
                    for n in range(BANKS):
                        act.wait_ge(b_done, s.after(BANKS, n + 1))
                        if past(count := s.after(BANKS, n - 2)):
                            act.wait_ge(pv_done, count)
                        nc.scalar.activation(prob[n % 3][:, :, :].rearrange("p h q -> p (h q)"), bank_s[n % 2][:, :],
                                             ACT.Exp).then_inc(prob_ready, 1)

            act.wait_ge(dve_consts, 1)
            schedule(act, body)

        @block.vector
        def _(dve):
            dve.wait_ge(consts_loaded, 16 * CONSTS)
            chain = sem("dve_const_chain")
            steps = [0]

            def const(instruction):
                steps[0] += 1
                instruction.then_inc(chain, 1)
                dve.wait_ge(chain, steps[0])

            const(nc.vector.memset(bias_p[:, :], 0.0))
            const(nc.vector.tensor_copy(bias_p[0:1, :], bias))
            const(nc.vector.tensor_tensor(bias_rest, bias, bias_p[0:1, :], ALU.subtract))
            part1 = parts[0:1, 0, 0:2, :].rearrange("p a n -> p (a n)")
            const(nc.vector.tensor_copy(part1, bias_rest))
            const(nc.vector.tensor_copy(bias_p[32:33, :], part1))
            const(nc.vector.tensor_tensor(bias, bias_rest, part1, ALU.subtract))
            const(nc.vector.tensor_copy(bias_p[64:65, :], bias))
            const(nc.vector.scalar_tensor_tensor(qk_scale[:, :], qn_col[:, :], SCALE, kn_col[:, :],
                                                 ALU.mult, ALU.mult))
            const(nc.vector.tensor_scalar(one_minus_mu[:, :, :], mu_col[:, :, :], -1.0, 1.0, ALU.mult, ALU.add))
            for i in range(2):
                const(nc.vector.memset(k_st[i][STACK:ROWS, :, :], 1.0))
                const(nc.vector.memset(v_own[i][:, :, :, :], 1.0))
                const(nc.vector.memset(v_mix[i][:, :, :, :], 1.0))
                const(nc.vector.memset(v_mix[i][0:WINDOW, 0, :, :], 0.0))
                const(nc.vector.memset(bank_o[i][:, :], 0.0))
            const(nc.vector.memset(x2T[:, :, 0:1], 0.0))
            nc.vector.memset(o_nrm[:, :, :], 0.0).then_inc(dve_consts, 1)
            dve.wait_ge(dve_consts, 1)

            def layernorm(src, s, st, mv, rstd, stats, mv_ready, rstd_ready, ready):
                for t in range(TILES):
                    nc.vector.bn_stats(st[:, t, :], src[:, t, :]).then_inc(stats, 1)
                for t in range(TILES):
                    if past(count := s.after(TILES, t + 1)):
                        count = held(dve, count)
                        dve.wait_ge(dve_consts, 1)
                        dve.wait_ge(stats, count)
                    nc.vector.bn_aggr(mv[:, t, :], st[:, t, :]).then_inc(mv_ready, 1)
                dve.wait_ge(rstd_ready, s.after(1, 1))
                for t in range(TILES):
                    nc.vector.tensor_scalar(xn[:, t, :], src[:, t, :], mv[:, t, 0:1], rstd[:, t:t + 1],
                                            ALU.subtract, ALU.mult).then_inc(ready, 1)

            def maxima(s, banks):
                for n in banks:
                    t, c = n // 4, n % 4
                    dve.wait_ge(a_done, s.after(BANKS, n + 1))
                    if n == 0:
                        if past(count := s.after(1, 0)):
                            dve.wait_ge(maxT_done, count)
                    nc.vector.tensor_reduce(smax[:, t, 4 * c:4 * c + 4],
                                            bank_s[n % 2][:, :].rearrange("p (h k) -> p h k", h=4),
                                            AX.X, ALU.max).then_inc(max_ready, 1)

            def body(s, attend, front, ffn):
                f, g = s.shifted(1), s.shifted(-1)
                if ffn:
                    dve.wait_ge(x1_ready, g.after(TILES, TILES))
                    dve.wait_ge(xT_done, g.after(KT, 2 * KT) if front or attend else g.after(KT, KT))
                    layernorm(x1, g, st2, mv2, rstd2, ln2_stats, ln2_mv, ln2_rstd, xn2_ready)
                if attend:
                    maxima(s, range(0, BANKS // 2))
                if front:
                    dve.wait_ge(x_loaded[f.parity], f.after_half(16, 16))
                    if past(count := f.after(KT, -KT)):
                        dve.wait_ge(x2T_done, count)
                    layernorm(x_in[f.parity], f, st1, mv1, rstd1, ln1_stats, ln1_mv, ln1_rstd, xn1_ready)
                if attend:
                    maxima(s, range(BANKS // 2, BANKS))
                if front:
                    for t in range(TILES):
                        dve.wait_ge(qk_done, f.after(TILES, t + 1))
                        if t == 0:
                            if past(count := f.after(TILES, 0)):
                                dve.wait_ge(qkT_done, count)
                        nc.vector.tensor_scalar(qk[:, t, :], bank_p[0][:, :], -CLIP, CLIP, ALU.max, ALU.min)\
                            .then_inc(qk_clipped, 1)
                        dve.wait_ge(sq_ready, f.after(TILES, t + 1))
                        nc.vector.tensor_reduce(rms[:, t, :], sq[t % 2][:, :].rearrange("p (h d) -> p h d", d=HD),
                                                AX.X, ALU.add).then_inc(sumsq_ready, 1)
                if attend:
                    dve.wait_ge(maxT_done, s.after(1, 1))
                    dve.wait_ge(neg0_ready, s.after(1, 1))
                    if past(count := s.after(1, 0)):
                        dve.wait_ge(neg2_ready, count)
                    nc.vector.scalar_tensor_tensor(neg_rest[:, :], bank_t[0][0:HEADS, :], -1.0, neg_p[0][:, :],
                                                   ALU.mult, ALU.subtract).then_inc(neg_rest_ready, 1)
                if ffn:
                    for c in range(2 * KT):
                        which, k = c // KT, c % KT
                        dve.wait_ge(mixa_ready, g.after(2 * KT, c + 1))
                        if c == 0:
                            if past(count := g.after(TILES, 0)):
                                dve.wait_ge(r_done, count)
                        nc.vector.scalar_tensor_tensor((xr, xk)[which][:, k, :], x2T[:, k, 1:L + 1],
                                                       mu_col[:, which, k:k + 1], mixa[c % 2][:, :],
                                                       ALU.mult, ALU.add).then_inc(mixed, 1)
                if front:
                    for t in range(TILES):
                        if t == 0:
                            dve.wait_ge(rms_ready, f.after(1, 1))
                            dve.wait_ge(qk_clipped, f.after(TILES, TILES))
                            dve.wait_ge(sq_ready, f.after(TILES, TILES))
                        q4 = qk[:, t, :].rearrange("p (h d) -> p h d", d=HD)
                        r4 = rms[:, t, :].rearrange("p (h o) -> p h o", o=1).broadcast_to([P, 2 * HEADS, HD])
                        nc.vector.tensor_tensor(q4, q4, r4, ALU.mult).then_inc(qkn_ready, 1)
                    for t in range(TILES):
                        dve.wait_ge(part0_ready, f.after(TILES, t + 1))
                        if past(count := f.after(TILES, t - 1)):
                            dve.wait_ge(part2_ready, count)
                        b4 = bank_t[t % 2][:, :].rearrange("p (b n) -> p b n", b=4)
                        cols = slice(P * t, P * t + P)
                        nc.vector.scalar_tensor_tensor(rest[t % 2][:, 0:2, :], b4[:, 0:2, :], qk_scale[:, :],
                                                       parts[:, 0:2, 0, cols], ALU.mult, ALU.subtract)
                        nc.vector.tensor_tensor(rest[t % 2][:, 2:4, :], b4[:, 2:4, :], parts[:, 2:4, 0, cols],
                                                ALU.subtract).then_inc(rest_ready, 1)
                if ffn:
                    for t in range(TILES):
                        dve.wait_ge(kv_done, g.after(TILES, t + 1))
                        dve.wait_ge(gate_ready, g.after(TILES, t + 1))
                        nc.vector.scalar_tensor_tensor(gate[:, t, :], gate[:, t, :], 1.0, bank_p[t % 2][:, 0:D],
                                                       ALU.add, ALU.mult).then_inc(kvr_ready, 1)
                        dve.wait_ge(kvr_ready, g.after(TILES, t + 1))
                        if t == 0:
                            if past(count := g.after(16, 0)):
                                dve.wait_ge(y_stored, count)
                        nc.vector.scalar_tensor_tensor(y[:, t, :], gate[:, t, :], 0.5, x1[:, t, :],
                                                       ALU.mult, ALU.add).then_inc(y_ready, 1)
                if attend:
                    for t in range(TILES):
                        dve.wait_ge(pv_done, s.after(BANKS, 4 * t + 4))
                        if past(count := s.after(TILES, t)):
                            dve.wait_ge(o_normed, count)
                        nc.vector.transpose(o_tok[:, :, :].rearrange("p c r -> p (c r)"), bank_o[t % 2][:, :])\
                            .then_inc(o_turned, 1)
                        dve.wait_ge(o_turned, s.after(TILES, t + 1))
                        nc.vector.reciprocal(o_inv[:, :], o_tok[:, :, HD]).then_inc(o_inverse, 1)
                        dve.wait_ge(o_inverse, s.after(TILES, t + 1))
                        if past(count := s.after(TILES, t)):
                            dve.wait_ge(oT_ready, count)
                        nc.vector.tensor_tensor(
                            o_nrm[:, :, 0:HD], o_tok[:, :, 0:HD],
                            o_inv[:, :].rearrange("p (c o) -> p c o", o=1).broadcast_to([P, 16, HD]),
                            ALU.mult).then_inc(o_normed, 1)
                        dve.wait_ge(o_normed, s.after(TILES, t + 1))
                        if t == 0:
                            if past(count := s.after(TILES, 0)):
                                dve.wait_ge(wo_done, count)
                        nc.vector.transpose(oT[:, t, :, :].rearrange("p b n -> p (b n)"),
                                            o_nrm[:, :, :].rearrange("p c r -> p (c r)")).then_inc(oT_ready, 1)
                    for t in range(TILES):
                        dve.wait_ge(wo_done, s.after(TILES, t + 1))
                        if t == 0:
                            if past(count := s.after(TILES, 0)):
                                dve.wait_ge(y_ready, count)
                            if past(count := s.after(TILES, 0)):
                                dve.wait_ge(xn2_ready, count)
                        nc.vector.tensor_tensor(x1[:, t, :], x_in[s.parity][:, t, :], bank_p[t % 2][:, 0:D],
                                                ALU.add).then_inc(x1_ready, 1)

            schedule(dve, body)

        @block.tensor
        def _(pe):
            pe.wait_ge(pool_consts, 1)
            pe.wait_ge(dve_consts, 1)
            pe.wait_ge(consts_loaded, 16 * CONSTS)

            def add_bias(dst, lo, n):
                nc.tensor.matmul(dst, ones_rows[:, :], bias_p[:, lo:lo + n], start=True, stop=False)

            def transposes(done):
                for k in range(KT):
                    for t in range(TILES):
                        last = nc.tensor.transpose(bank_t[k][:, P * t:P * t + P], xn[:, t, P * k:P * k + P],
                                                   ident[:, :])
                    last.then_inc(done, 1)

            def scores_a(s, banks):
                q, k = q_st[s.parity], k_st[s.parity]
                for n in banks:
                    t, c = n // 4, n % 4
                    dst = bank_s[n % 2]
                    if n < 2:
                        if past(count := s.after(BANKS, n - 1 if n == 0 else 0)):
                            pe.wait_ge(prob_ready, count)
                    else:
                        pe.wait_ge(max_ready, s.after(BANKS, n - 1))
                    nc.tensor.matmul(dst[:, :], ident_b[:, :],
                                     mask_a[min(t, 1)][:, :, :].rearrange("p h k -> p (h k)"),
                                     start=True, stop=False, skip_group_check=True)
                    for j in range(4):
                        for half in range(2):
                            h, i = 4 * c + j, 2 * t + half
                            lo = max(0, WINDOW * (i - 1))
                            hi = WINDOW * (i + 1)
                            last = nc.tensor.matmul(
                                dst[WINDOW * half:WINDOW * half + WINDOW, P * (j + 1) - (hi - lo):P * (j + 1)],
                                q[0:STACK, h, WINDOW * i:hi], k[0:STACK, h, lo:hi],
                                start=False, stop=True, skip_group_check=True)
                    last.then_inc(a_done, 1)

            def scores_b(s, n):
                q, k = q_st[s.parity], k_st[s.parity]
                i, c = n // 2, n % 2
                dst = bank_s[n % 2]
                if n < 2:
                    pe.wait_ge(max_ready, s.after(BANKS, BANKS))
                else:
                    pe.wait_ge(prob_ready, s.after(BANKS, n - 1))
                nc.tensor.matmul(dst[:, :], ident_b[:, :],
                                 mask_b[min(i, 1)][:, :, :].rearrange("p h q -> p (h q)"),
                                 start=True, stop=False, skip_group_check=True)
                for j in range(8):
                    h = 8 * c + j
                    lo, hi = max(0, WINDOW * (i - 1)), WINDOW * (i + 1)
                    last = nc.tensor.matmul(dst[P - (hi - lo):P, WINDOW * j:WINDOW * j + WINDOW],
                                            k[0:ROWS, h, lo:hi], q[0:ROWS, h, WINDOW * i:hi],
                                            start=False, stop=True, skip_group_check=True)
                last.then_inc(b_done, 1)

            def times_v(s, n):
                i, c = n // 2, n % 2
                t = i // 2
                v = v_own[s.parity] if i % 2 else v_mix[s.parity]
                pe.wait_ge(prob_ready, s.after(BANKS, n + 1))
                if n % 4 == 0:
                    if past(count := s.after(TILES, t - 1)):
                        pe.wait_ge(o_turned, count)
                for j in range(8):
                    h = 8 * c + j
                    quad, row = h // 4, 32 * (h % 4)
                    col = P * quad + WINDOW * (i % 2)
                    last = nc.tensor.matmul(bank_o[t % 2][row:row + HD + 1, col:col + WINDOW],
                                            v[:, t, h, :], prob[n % 3][:, j, :], start=True, stop=True,
                                            tile_position=(0, row))
                last.then_inc(pv_done, 1)

            def body(s, attend, front, ffn):
                f, g = s.shifted(1), s.shifted(-1)
                if attend:
                    pe.wait_ge(stack_loaded[s.parity], s.after_half(16 * 12, 16 * 12))
                    scores_a(s, range(0, BANKS // 2))
                if ffn:
                    pe.wait_ge(xn2_ready, g.after(TILES, TILES))
                    pe.wait_ge(part0_ready, s.after(TILES, TILES) if attend else g.after(TILES, TILES))
                    pe.wait_ge(rest_ready, s.after(TILES, TILES) if attend else g.after(TILES, TILES))
                    transposes(x2T_done)
                if front:
                    pe.wait_ge(xn1_ready, f.after(TILES, TILES))
                    if ffn:
                        pe.wait_ge(x2T_ready, g.after(KT, KT))
                    else:
                        if past(count := s.after(TILES, TILES)):
                            pe.wait_ge(part0_ready, count)
                        if past(count := s.after(TILES, TILES)):
                            pe.wait_ge(rest_ready, count)
                    transposes(xT_done)
                if attend:
                    scores_a(s, range(BANKS // 2, BANKS))
                if front:
                    pe.wait_ge(xT_ready, f.after(KT, KT))
                    for t in range(TILES):
                        cols = slice(P * t, P * t + P)
                        if t:
                            pe.wait_ge(qk_clipped, f.after(TILES, t))
                        else:
                            if past(count := s.after(TILES, 0)):
                                pe.wait_ge(x1_ready, count)
                        add_bias(bank_p[0][:, :], 0, 2 * D)
                        for k in range(KT):
                            last = nc.tensor.matmul(bank_p[0][:, :], xT[:, k, cols], w_qk[:, k, :],
                                                    start=False, stop=(k == KT - 1))
                        last.then_inc(qk_done, 1)
                        if t:
                            pe.wait_ge(v_ready, f.after(TILES, t))
                        add_bias(bank_p[1][:, 0:D], 2 * D, D)
                        for k in range(KT):
                            last = nc.tensor.matmul(bank_p[1][:, 0:D], xT[:, k, cols], w_v[:, k, :],
                                                    start=False, stop=(k == KT - 1))
                        last.then_inc(v_done, 1)
                if attend:
                    pe.wait_ge(max_ready, s.after(BANKS, BANKS))
                    if front:
                        pe.wait_ge(xT_ready, f.after(KT, KT))
                    elif ffn:
                        pe.wait_ge(x2T_ready, g.after(KT, KT))
                    for t in range(TILES):
                        last = nc.tensor.transpose(bank_t[0][0:HEADS, P * t:P * t + P], smax[:, t, :], ident[:, :])
                    last.then_inc(maxT_done, 1)
                if ffn:
                    pe.wait_ge(mixed, g.after(2 * KT, 2 * KT))
                    pe.wait_ge(x2T_ready, g.after(KT, KT))
                    if attend:
                        pe.wait_ge(neg0_ready, s.after(1, 1))
                        pe.wait_ge(neg_rest_ready, s.after(1, 1))
                    for m in range(KT):
                        for k in range(KT):
                            last = nc.tensor.matmul(bank_t[m][:, :], w_k[:, k, P * m:P * m + P], xk[:, k, :],
                                                    start=(k == 0), stop=(k == KT - 1))
                        last.then_inc(k_done, 1)
                    for t in range(TILES):
                        if t == 0:
                            if front:
                                pe.wait_ge(qk_clipped, f.after(TILES, TILES))
                                pe.wait_ge(v_ready, f.after(TILES, TILES))
                            else:
                                pe.wait_ge(x1_ready, g.after(TILES, TILES))
                        else:
                            if past(count := g.after(TILES, t - 1)):
                                pe.wait_ge(gate_ready, count)
                        for k in range(KT):
                            last = nc.tensor.matmul(bank_p[t % 2][:, 0:D], xr[:, k, P * t:P * t + P], w_r[:, k, :],
                                                    start=(k == 0), stop=(k == KT - 1))
                        last.then_inc(r_done, 1)
                if front:
                    for t in range(TILES):
                        pe.wait_ge(qkn_ready, f.after(TILES, t + 1))
                        if t == 0:
                            if ffn:
                                pe.wait_ge(relu_ready, g.after(KT, KT))
                            elif attend:
                                pe.wait_ge(neg0_ready, s.after(1, 1))
                                pe.wait_ge(neg_rest_ready, s.after(1, 1))
                        elif t >= 2:
                            pe.wait_ge(part0_ready, f.after(TILES, t - 1))
                            pe.wait_ge(rest_ready, f.after(TILES, t - 1))
                        for b in range(4):
                            last = nc.tensor.transpose(bank_t[t % 2][:, P * b:P * b + P], qk[:, t, P * b:P * b + P],
                                                       ident[:, :])
                        last.then_inc(qkT_done, 1)
                if ffn:
                    pe.wait_ge(kact_ready, g.after(KT, KT))
                    for t in range(TILES):
                        if t == 0:
                            pe.wait_ge(gate_ready, g.after(TILES, TILES))
                        else:
                            if past(count := g.after(TILES, t - 1)):
                                pe.wait_ge(kvr_ready, count)
                        for k in range(KT):
                            last = nc.tensor.matmul(bank_p[t % 2][:, 0:D], kact[:, k, P * t:P * t + P], w_f[:, k, :],
                                                    start=(k == 0), stop=(k == KT - 1))
                        last.then_inc(kv_done, 1)
                if attend:
                    pe.wait_ge(max_rows_loaded, s.after(16 * PARTS, 16 * PARTS))
                    for n in range(BANKS):
                        scores_b(s, n)
                        if n:
                            times_v(s, n - 1)
                    times_v(s, BANKS - 1)
                    for t in range(TILES):
                        pe.wait_ge(oT_ready, s.after(TILES, t + 1))
                        if t == 0:
                            if ffn:
                                pe.wait_ge(kvr_ready, g.after(TILES, TILES))
                            elif front:
                                pe.wait_ge(qk_clipped, f.after(TILES, TILES))
                                pe.wait_ge(v_ready, f.after(TILES, TILES))
                        elif t >= 2:
                            pe.wait_ge(x1_ready, s.after(TILES, t - 1))
                        add_bias(bank_p[t % 2][:, 0:D], 3 * D, D)
                        for quad in range(QUADS):
                            last = nc.tensor.matmul(bank_p[t % 2][:, 0:D], oT[:, t, quad, :], w_o[:, quad, :],
                                                    start=False, stop=(quad == QUADS - 1))
                        last.then_inc(wo_done, 1)

            schedule(pe, body)


def kernel(L0_attn_x, L0_attn_wq_w, L0_attn_wq_b, L0_attn_wk_w, L0_attn_wk_b, L0_attn_wv_w, L0_attn_wv_b,
           L0_attn_wo_w, L0_attn_wo_b, L0_attn_qn_w, L0_attn_kn_w, L0_ffn_W_r, L0_ffn_W_k, L0_ffn_W_v,
           L0_ffn_mu_r, L0_ffn_mu_k):
    import concourse.bacc as bacc
    from concourse.bass_utils import run_bass_kernel_spmd

    wo = np.zeros((HEADS, 2 * HD, D), np.float32)
    wo[:, 0:HD, :] = np.asarray(L0_attn_wo_w).T.reshape(HEADS, HD, D)
    arrays = {
        "x": np.asarray(L0_attn_x).reshape(SEQS * L, D),
        "wqkT": np.concatenate([np.asarray(L0_attn_wq_w).T, np.asarray(L0_attn_wk_w).T], axis=1),
        "wvT": np.asarray(L0_attn_wv_w).T,
        "woP": wo.reshape(HEADS * 2 * HD, D),
        "wrT": np.asarray(L0_ffn_W_r).T,
        "wkT": np.asarray(L0_ffn_W_k).T,
        "wfT": np.asarray(L0_ffn_W_v).T,
        "bqkv": np.concatenate([np.asarray(L0_attn_wq_b), np.asarray(L0_attn_wk_b),
                                np.asarray(L0_attn_wv_b)]).reshape(1, 3 * D),
        "bo": np.asarray(L0_attn_wo_b).reshape(1, D),
        "qn": np.tile(np.asarray(L0_attn_qn_w), P // HD).reshape(P, 1),
        "kn": np.tile(np.asarray(L0_attn_kn_w), P // HD).reshape(P, 1),
        "mu": np.stack([np.asarray(L0_ffn_mu_r).reshape(KT, P), np.asarray(L0_ffn_mu_k).reshape(KT, P)])
        .transpose(2, 0, 1),
    }
    arrays = {k: np.ascontiguousarray(v) for k, v in arrays.items()}
    nc = bacc.Bacc("TRN2", target_bir_lowering=False, num_devices=1)
    ins = [nc.dram_tensor(k, v.shape, FP32, kind="ExternalInput").ap() for k, v in arrays.items()]
    out = nc.dram_tensor("out", (SEQS * L, D), FP32, kind="ExternalOutput").ap()
    build(nc, *ins, out)
    r = run_bass_kernel_spmd(nc, [arrays], core_ids=[0])
    return r.results[0]["out"].reshape(SEQS, L, D)
```

```python
from contextlib import ExitStack

import numpy as np
import concourse.bass as bass
from concourse import mybir

FP32 = mybir.dt.float32
BF16 = mybir.dt.bfloat16
ALU = mybir.AluOpType
ACT = mybir.ActivationFunctionType
AX = mybir.AxisListType

SEQS, L, D = 32, 512, 256
HEADS, HD = 16, 16
WINDOW = 64
P = 128
TILES = L // P
KT = D // P
BLOCKS = L // WINDOW
PARTS = 3
Q_SLOTS = (0, 0, 0, 1, 1, 2)
K_SLOTS = (0, 1, 2, 0, 1, 0)
STACK = HD * len(Q_SLOTS)
ROWS = STACK + PARTS
LN_EPS = 1e-5
RMS_EPS = 1e-5
CLIP = 1e4
SCALE = float(HD) ** -0.5
MASKED = -1e30
QUADS = HEADS // 4


class Seq:

    def __init__(self, pair, offset):
        self.pair, self.offset = pair, offset
        self.n = 2 * pair + offset
        self.parity = offset % 2
        self.half = pair + offset // 2

    def shifted(self, by):
        return Seq(self.pair, self.offset + by)

    def after(self, per, k):
        return self.n * per + k

    def after_half(self, per, k):
        return self.half * per + k


def past(count):
    return not isinstance(count, int) or count > 0


def held(eng, count):
    return count if isinstance(count, int) else eng.to_reg(count)


def build(nc, x, wqkT, wvT, woP, wrT, wkT, wfT, bqkv, bo, qn, kn, mu, out):
    ctx = ExitStack()
    with ctx:
        def sb(name, shape, dt=FP32):
            return ctx.enter_context(nc.sbuf_tensor(name, shape, dt))

        def ps(name):
            return ctx.enter_context(nc.psum_tensor(name, [P, 512], FP32))

        def sem(name):
            return ctx.enter_context(nc.semaphore(name))

        w_qk = sb("w_qk", [P, KT, 2 * D])
        w_v = sb("w_v", [P, KT, D])
        w_o = sb("w_o", [P, KT, D])
        w_r = sb("w_r", [P, KT, D])
        w_k = sb("w_k", [P, KT, D])
        w_f = sb("w_f", [P, KT, D])
        bias_p = sb("bias_p", [65, 4 * D], BF16)
        ones_rows = sb("ones_rows", [65, P], BF16)
        qn_col = sb("qn_col", [P, 1])
        kn_col = sb("kn_col", [P, 1])
        qk_scale = sb("qk_scale", [P, 1])
        mu_col = sb("mu_col", [P, 2, KT])
        one_minus_mu = sb("one_minus_mu", [P, 2, KT])
        minus_half = sb("minus_half", [P, TILES])
        ident = sb("ident", [P, P])
        ident_b = sb("ident_b", [P, P], BF16)
        mask_a = [sb(f"mask_a{i}", [P, 4, P], BF16) for i in range(2)]
        mask_b = [sb(f"mask_b{i}", [P, 8, WINDOW], BF16) for i in range(2)]

        x_in = sb("x_in", [P, TILES, D])
        xn1 = sb("xn1", [P, TILES, D])
        xn2 = sb("xn2", [P, TILES, D])
        xT = sb("xT", [P, KT, L])
        qk = sb("qk", [P, TILES, 2 * D])
        bias = qk[0:1, 0:2, :].rearrange("p a n -> p (a n)")
        bias_rest = qk[0:1, 2:4, :].rearrange("p a n -> p (a n)")
        sq = [sb(f"sq{i}", [P, 2 * D]) for i in range(2)]
        rms_v = sb("rms_v", [P, TILES * 2 * HEADS])
        rms_r = sb("rms_r", [P, TILES * 2 * HEADS])
        rms_w = sb("rms_w", [P, TILES * 2 * HEADS])
        parts = sb("parts", [P, 4, PARTS, L], BF16)
        rest = [sb(f"rest{i}", [P, 4, P]) for i in range(2)]
        q_st = [sb(f"q_st{i}", [P, HEADS, L], BF16) for i in range(2)]
        k_st = [sb(f"k_st{i}", [P, HEADS, L], BF16) for i in range(2)]
        v_own = [sb(f"v_own{i}", [P, TILES, HEADS, HD + 1]) for i in range(2)]
        v_mix = [sb(f"v_mix{i}", [P, TILES, HEADS, HD + 1]) for i in range(2)]
        smax = sb("smax", [P, TILES, HEADS])
        neg_rest = sb("neg_rest", [HEADS, L])
        neg_p = [sb(f"neg_p{i}", [HEADS, L], BF16) for i in range(PARTS)]
        prob = [sb(f"prob{i}", [P, 8, WINDOW]) for i in range(3)]
        o_tok = sb("o_tok", [P, 16, 32])
        o_inv = sb("o_inv", [P, 16])
        o_nrm = sb("o_nrm", [P, KT, 4, 32])
        oT = sb("oT", [P, TILES, KT, P])
        x1 = [sb(f"x1_{i}", [P, TILES, D]) for i in range(2)]
        x2T = sb("x2T", [P, KT, L + 1])
        xr = sb("xr", [P, KT, L])
        xk = sb("xk", [P, KT, L])
        kact = sb("kact", [P, KT, L])
        gate = sb("gate", [P, TILES, D])
        st1 = sb("st1", [P, TILES, 6])
        mv1 = sb("mv1", [P, TILES, 2])
        rstd1 = sb("rstd1", [P, TILES])
        st2 = sb("st2", [P, TILES, 6])
        mv2 = sb("mv2", [P, TILES, 2])
        rstd2 = sb("rstd2", [P, TILES])

        bank_t = [ps(f"bank_t{i}") for i in range(2)]
        bank_p = [ps(f"bank_p{i}") for i in range(2)]
        bank_s = [ps(f"bank_s{i}") for i in range(2)]
        bank_o = [ps(f"bank_o{i}") for i in range(2)]

        scratch = [nc.dram_tensor(f"scratch{i}", (2, D, PARTS, L), BF16).ap() for i in range(2)]

        def sems(*names):
            return [sem(n) for n in names]

        consts_loaded, x_loaded, res_loaded, y_stored, scratch_written, max_rows_loaded = sems(
            "consts_loaded", "x_loaded", "res_loaded", "y_stored", "scratch_written", "max_rows_loaded")
        stack_loaded = [sem(f"stack_loaded{i}") for i in range(2)]
        pool_consts, pool_step, ln1_eps, ln1_rstd, ln2_eps, ln2_rstd, rms_step, rms_ready, part2_ready, neg2_ready = sems(
            "pool_consts", "pool_step", "ln1_eps", "ln1_rstd", "ln2_eps", "ln2_rstd", "rms_step", "rms_ready",
            "part2_ready", "neg2_ready")
        dve_consts, dve_step, ln1_stats, ln1_mv, xn1_ready, ln2_stats, ln2_mv, xn2_ready = sems(
            "dve_consts", "dve_step", "ln1_stats", "ln1_mv", "xn1_ready", "ln2_stats", "ln2_mv", "xn2_ready")
        qk_clipped, sumsq_ready, rms_seed, qkn_ready, rest_ready, max_ready, neg_rest_ready = sems(
            "qk_clipped", "sumsq_ready", "rms_seed", "qkn_ready", "rest_ready", "max_ready", "neg_rest_ready")
        mixed, kvr_ready, y_ready, o_turned, o_inverse, o_normed, oT_ready, x1_ready = sems(
            "mixed", "kvr_ready", "y_ready", "o_turned", "o_inverse", "o_normed", "oT_ready", "x1_ready")
        xT_ready, sq_ready, v_ready, part0_ready, part1_ready, neg0_ready, neg1_ready = sems(
            "xT_ready", "sq_ready", "v_ready", "part0_ready", "part1_ready", "neg0_ready", "neg1_ready")
        x2T_ready, mixa_ready, relu_ready, kact_ready, gate_ready, prob_ready = sems(
            "x2T_ready", "mixa_ready", "relu_ready", "kact_ready", "gate_ready", "prob_ready")
        xT_done, qk_done, v_done, qkT_done, a_done, maxT_done, b_done, pv_done, wo_done = sems(
            "xT_done", "qk_done", "v_done", "qkT_done", "a_done", "maxT_done", "b_done", "pv_done", "wo_done")
        x2T_done, k_done, r_done, kv_done = sems("x2T_done", "k_done", "r_done", "kv_done")

        CONSTS = 11
        BANKS = TILES * HEADS // 4

        NEWTON = 3
        RMS_STEPS = 3 + 4 * NEWTON - 1

        def schedule(eng, body):
            body(Seq(0, -2), True, False, False, False)
            body(Seq(0, -1), True, True, False, False)
            body(Seq(0, 0), True, True, True, False)
            body(Seq(0, 1), True, True, True, True)
            with eng.Fori(0, (SEQS - 4) // 2) as pair:
                body(Seq(pair, 2), True, True, True, True)
                body(Seq(pair, 3), True, True, True, True)
            body(Seq(0, SEQS - 2), False, True, True, True)
            body(Seq(0, SEQS - 1), False, False, True, True)
            body(Seq(0, SEQS), False, False, False, True)

        block = ctx.enter_context(nc.Block())

        @block.sync
        def _(sp):
            for dst, src in ((w_qk, wqkT), (w_v, wvT), (w_r, wrT), (w_k, wkT), (w_f, wfT)):
                sp.dma_start(dst[:, :, :], src.rearrange("(k p) n -> p k n", p=P)).then_inc(consts_loaded, 16)
            sp.dma_start(w_o[:, :, :], woP.rearrange("(k p) n -> p k n", p=P)).then_inc(consts_loaded, 16)
            sp.dma_start(bias[:, 0:3 * D], bqkv).then_inc(consts_loaded, 16)
            sp.dma_start(bias[:, 3 * D:4 * D], bo).then_inc(consts_loaded, 16)
            sp.dma_start(qn_col[:, :], qn).then_inc(consts_loaded, 16)
            sp.dma_start(kn_col[:, :], kn).then_inc(consts_loaded, 16)
            sp.dma_start(mu_col[:, :, :], mu).then_inc(consts_loaded, 16)

            def rows(dram, s):
                return dram[bass.ds(s.n * L, L), :].rearrange("(t p) d -> p t d", p=P)

            def body(s, lead, front, attend, ffn):
                e, f, g = s.shifted(2), s.shifted(1), s.shifted(-1)
                if attend:
                    if past(count := g.after(16, 0)):
                        count = held(sp, count)
                        sp.wait_ge(consts_loaded, 16 * CONSTS)
                        sp.wait_ge(y_stored, count)
                    sp.dma_start(x1[s.parity][:, :, :], rows(x, s)).then_inc(res_loaded, 16)
                if lead:
                    if past(count := e.after(TILES, 0)):
                        count = held(sp, count)
                        sp.wait_ge(consts_loaded, 16 * CONSTS)
                        sp.wait_ge(xn1_ready, count)
                    sp.dma_start(x_in[:, :, :], rows(x, e)).then_inc(x_loaded, 16)
                if attend:
                    sp.wait_ge(neg0_ready, s.after(1, 1))
                    sp.wait_ge(neg1_ready, s.after(1, 1))
                    sp.wait_ge(neg2_ready, s.after(1, 1))
                    for i in range(PARTS):
                        sp.dma_start(q_st[s.parity][STACK + i:STACK + i + 1, :, :], neg_p[i][:, :])\
                            .then_inc(max_rows_loaded, 16)
                if front:
                    sp.wait_ge(part0_ready, f.after(TILES, TILES))
                    sp.wait_ge(part1_ready, f.after(TILES, TILES))
                    sp.wait_ge(part2_ready, f.after(TILES, TILES))
                    sp.dma_start(scratch[f.parity].rearrange("w (g p) a t -> p (w g) (a t)", p=P),
                                 parts[:, :, :, :].rearrange("p b a t -> p b (a t)")).then_inc(scratch_written, 16)
                    if past(count := f.after(BANKS, -BANKS)):
                        count = held(sp, count)
                        sp.wait_ge(consts_loaded, 16 * CONSTS)
                        sp.wait_ge(b_done, count)
                    count = held(sp, f.after(16, 16))
                    sp.wait_ge(consts_loaded, 16 * CONSTS)
                    sp.wait_ge(scratch_written, count)
                    for st, which, slots in ((q_st, 0, Q_SLOTS), (k_st, 1, K_SLOTS)):
                        for slot, part in enumerate(slots):
                            src = scratch[f.parity][which, :, part, :].rearrange("(h r) t -> r h t", r=HD)
                            sp.dma_start(st[f.parity][HD * slot:HD * slot + HD, :, :], src)\
                                .then_inc(stack_loaded[f.parity], 16)
                if ffn:
                    count = held(sp, g.after(TILES, TILES))
                    sp.wait_ge(consts_loaded, 16 * CONSTS)
                    sp.wait_ge(y_ready, count)
                    sp.dma_start(rows(out, g), x1[g.parity][:, :, :]).then_inc(y_stored, 16)

            schedule(sp, body)
            sp.wait_ge(y_stored, 16 * SEQS)

        @block.gpsimd
        def _(pool):
            steps = [0]

            def const(instruction):
                steps[0] += 1
                instruction.then_inc(pool_step, 1)
                pool.wait_ge(pool_step, steps[0])

            def fill_mask(m, rows, pattern, base, per_row):
                view = m[rows[0]:rows[1], :, :]
                const(nc.gpsimd.affine_select(out=view, in_=view, compare_op=ALU.is_ge, fill=MASKED,
                                              base=base, pattern=pattern, channel_multiplier=per_row))

            for m in (ident, ident_b):
                const(nc.gpsimd.memset(m[:, :], 0.0))
                const(nc.gpsimd.affine_select(out=m[:, :], in_=m[:, :], compare_op=ALU.not_equal, fill=1.0,
                                              base=0, pattern=[[-1, P]], channel_multiplier=1))
            for m in (*mask_a, *mask_b):
                const(nc.gpsimd.memset(m[:, :, :], 0.0))
            W = WINDOW
            for i, m in enumerate(mask_a):
                for half in range(2):
                    rows = (W * half, W * half + W)
                    fill_mask(m, rows, [[0, 4], [1, P]], -1, -1)
                    fill_mask(m, rows, [[0, 4], [-1, P]], W, 1)
                if i == 0:
                    fill_mask(m, (0, W), [[0, 4], [1, P]], -W, 0)
            for m in mask_b:
                fill_mask(m, (0, P), [[0, 8], [-1, W]], -1, 1)
                fill_mask(m, (0, P), [[0, 8], [1, W]], W, -1)
            fill_mask(mask_b[0], (0, W), [[0, 8], [0, W]], -1, 0)
            const(nc.gpsimd.memset(minus_half[:, :], -0.5))
            nc.gpsimd.memset(ones_rows[:, :], 1.0).then_inc(pool_consts, 1)

            def body(s, lead, front, attend, ffn):
                e, f, g = s.shifted(2), s.shifted(1), s.shifted(-1)
                if ffn:
                    count = held(pool, g.after(TILES, TILES))
                    pool.wait_ge(dve_consts, 1)
                    pool.wait_ge(ln2_mv, count)
                    nc.gpsimd.tensor_scalar(rstd2[:, :], mv2[:, :, 1], LN_EPS, None, ALU.add).then_inc(ln2_eps, 1)
                    pool.wait_ge(ln2_eps, g.after(1, 1))
                    nc.gpsimd.tensor_tensor(rstd2[:, :], rstd2[:, :], minus_half[:, :], ALU.pow).then_inc(ln2_rstd, 1)
                if front:
                    count = held(pool, f.after(TILES, TILES))
                    pool.wait_ge(dve_consts, 1)
                    pool.wait_ge(sumsq_ready, count)
                    nc.gpsimd.tensor_scalar(rms_v[:, :], rms_v[:, :], 1.0 / HD, RMS_EPS, ALU.mult, ALU.max)\
                        .then_inc(rms_step, 1)
                    count = held(pool, f.after(RMS_STEPS, 1))
                    pool.wait_ge(dve_consts, 1)
                    pool.wait_ge(rms_step, count)
                    nc.gpsimd.tensor_scalar(rms_v[:, :], rms_v[:, :], RMS_EPS, None, ALU.add).then_inc(rms_step, 1)
                    count = held(pool, f.after(1, 1))
                    pool.wait_ge(dve_consts, 1)
                    pool.wait_ge(rms_seed, count)
                    nc.gpsimd.tensor_scalar(rms_v[:, :], rms_v[:, :], -0.5, None, ALU.mult).then_inc(rms_step, 1)
                    for i in range(NEWTON):
                        pool.wait_ge(rms_step, f.after(RMS_STEPS, 3 + 4 * i))
                        nc.gpsimd.tensor_tensor(rms_w[:, :], rms_r[:, :], rms_r[:, :], ALU.mult).then_inc(rms_step, 1)
                        pool.wait_ge(rms_step, f.after(RMS_STEPS, 4 + 4 * i))
                        nc.gpsimd.tensor_tensor(rms_w[:, :], rms_w[:, :], rms_v[:, :], ALU.mult).then_inc(rms_step, 1)
                        count = held(pool, f.after(RMS_STEPS, 5 + 4 * i))
                        pool.wait_ge(dve_consts, 1)
                        pool.wait_ge(rms_step, count)
                        nc.gpsimd.tensor_scalar(rms_w[:, :], rms_w[:, :], 1.5, None, ALU.add).then_inc(rms_step, 1)
                        pool.wait_ge(rms_step, f.after(RMS_STEPS, 6 + 4 * i))
                        nc.gpsimd.tensor_tensor(rms_r[:, :], rms_r[:, :], rms_w[:, :], ALU.mult)\
                            .then_inc(rms_ready if i == NEWTON - 1 else rms_step, 1)
                if attend:
                    pool.wait_ge(neg_rest_ready, s.after(1, 1))
                    pool.wait_ge(neg1_ready, s.after(1, 1))
                    if past(count := s.after(16 * PARTS, 0)):
                        pool.wait_ge(max_rows_loaded, count)
                    nc.gpsimd.tensor_tensor(neg_p[2][:, :], neg_rest[:, :], neg_p[1][:, :], ALU.subtract)\
                        .then_inc(neg2_ready, 1)
                if front:
                    for t in range(TILES):
                        if t == 0:
                            if past(count := f.after(16, 0)):
                                pool.wait_ge(scratch_written, count)
                        pool.wait_ge(rest_ready, f.after(TILES, t + 1))
                        pool.wait_ge(part1_ready, f.after(TILES, t + 1))
                        nc.gpsimd.tensor_tensor(parts[:, :, 2, P * t:P * t + P], rest[t % 2][:, :, :],
                                                parts[:, :, 1, P * t:P * t + P], ALU.subtract)\
                            .then_inc(part2_ready, 1)
                if lead:
                    count = held(pool, e.after(TILES, TILES))
                    pool.wait_ge(dve_consts, 1)
                    pool.wait_ge(ln1_mv, count)
                    nc.gpsimd.tensor_scalar(rstd1[:, :], mv1[:, :, 1], LN_EPS, None, ALU.add).then_inc(ln1_eps, 1)
                    pool.wait_ge(ln1_eps, e.after(1, 1))
                    nc.gpsimd.tensor_tensor(rstd1[:, :], rstd1[:, :], minus_half[:, :], ALU.pow).then_inc(ln1_rstd, 1)

            schedule(pool, body)

        @block.scalar
        def _(act):
            def v_and_squares(f, t):
                act.wait_ge(v_done, f.after(TILES, t + 1))
                if t == 0:
                    if past(count := f.after(BANKS, -BANKS)):
                        act.wait_ge(pv_done, count)
                v4 = bank_p[1][:, 0:D].rearrange("p (h d) -> p h d", d=HD)
                own, mix = v_own[f.parity], v_mix[f.parity]
                nc.scalar.activation(own[:, t, :, 0:HD], v4, ACT.Copy)
                last = nc.scalar.activation(mix[WINDOW:P, t, :, 0:HD], v4[0:WINDOW], ACT.Copy)
                if t + 1 < TILES:
                    last = nc.scalar.activation(mix[0:WINDOW, t + 1, :, 0:HD], v4[WINDOW:P], ACT.Copy)
                last.then_inc(v_ready, 1)
                act.wait_ge(qk_clipped, f.after(TILES, t + 1))
                if past(count := f.after(TILES, t - 1)):
                    act.wait_ge(sumsq_ready, count)
                nc.scalar.activation(sq[t % 2][:, :], qk[:, t, :], ACT.Square).then_inc(sq_ready, 1)

            def body(s, lead, front, attend, ffn):
                f, g = s.shifted(1), s.shifted(-1)
                if front:
                    for k in range(KT):
                        act.wait_ge(xT_done, f.after(KT, k + 1))
                        if k == 0:
                            if past(count := f.after(TILES, 0)):
                                act.wait_ge(v_done, count)
                        nc.scalar.activation(xT[:, k, :], bank_t[k][:, :], ACT.Copy).then_inc(xT_ready, 1)
                    v_and_squares(f, 0)
                if ffn:
                    for k in range(KT):
                        act.wait_ge(x2T_done, g.after(KT, k + 1))
                        if k == 0:
                            if past(count := g.after(2 * KT, 0)):
                                act.wait_ge(mixed, count)
                        nc.scalar.activation(x2T[:, k, 1:L + 1], bank_t[k][:, :], ACT.Copy).then_inc(x2T_ready, 1)
                    for c in range(2 * KT):
                        which, k = c // KT, c % KT
                        act.wait_ge(x2T_ready, g.after(KT, KT))
                        if c == 0:
                            if past(count := g.after(TILES, 0)):
                                act.wait_ge(r_done, count)
                        nc.scalar.activation((xr, xk)[which][:, k, :], x2T[:, k, 0:L], ACT.Copy,
                                             scale=one_minus_mu[:, which, k:k + 1]).then_inc(mixa_ready, 1)
                if front:
                    for t in range(1, TILES):
                        v_and_squares(f, t)
                if ffn:
                    for m in range(KT):
                        act.wait_ge(k_done, g.after(KT, m + 1))
                        if m == 0:
                            if past(count := g.after(TILES, 0)):
                                act.wait_ge(kv_done, count)
                        nc.scalar.activation(kact[:, m, :], bank_t[m][:, :], ACT.Relu).then_inc(relu_ready, 1)
                if attend:
                    act.wait_ge(maxT_done, s.after(1, 1))
                    if past(count := s.after(16 * PARTS, 0)):
                        act.wait_ge(max_rows_loaded, count)
                    nc.scalar.activation(neg_p[0][:, :], bank_t[0][0:HEADS, :], ACT.Copy, scale=-1.0)\
                        .then_inc(neg0_ready, 1)
                if ffn:
                    for m in range(KT):
                        act.wait_ge(relu_ready, g.after(KT, m + 1))
                        nc.scalar.activation(kact[:, m, :], kact[:, m, :], ACT.Square).then_inc(kact_ready, 1)
                if attend:
                    act.wait_ge(neg_rest_ready, s.after(1, 1))
                    nc.scalar.activation(neg_p[1][:, :], neg_rest[:, :], ACT.Copy).then_inc(neg1_ready, 1)
                if ffn:
                    for t in range(TILES):
                        act.wait_ge(r_done, g.after(TILES, t + 1))
                        if t == 0:
                            if past(count := g.after(TILES, 0)):
                                act.wait_ge(y_ready, count)
                        nc.scalar.activation(gate[:, t, :], bank_p[t % 2][:, 0:D], ACT.Tanh, scale=0.5)\
                            .then_inc(gate_ready, 1)
                if front:
                    for t in range(TILES):
                        act.wait_ge(qkT_done, f.after(TILES, t + 1))
                        if t == 0:
                            if past(count := f.after(16, 0)):
                                act.wait_ge(scratch_written, count)
                        b4 = bank_t[t % 2][:, :].rearrange("p (b n) -> p b n", b=4)
                        cols = slice(P * t, P * t + P)
                        nc.scalar.activation(parts[:, 0:2, 0, cols], b4[:, 0:2, :], ACT.Copy, scale=qk_scale[:, :])
                        nc.scalar.activation(parts[:, 2:4, 0, cols], b4[:, 2:4, :], ACT.Copy).then_inc(part0_ready, 1)
                        act.wait_ge(rest_ready, f.after(TILES, t + 1))
                        nc.scalar.activation(parts[:, :, 1, cols], rest[t % 2][:, :, :], ACT.Copy)\
                            .then_inc(part1_ready, 1)
                if attend:
                    for n in range(BANKS):
                        act.wait_ge(b_done, s.after(BANKS, n + 1))
                        if past(count := s.after(BANKS, n - 2)):
                            act.wait_ge(pv_done, count)
                        nc.scalar.activation(prob[n % 3][:, :, :].rearrange("p h q -> p (h q)"), bank_s[n % 2][:, :],
                                             ACT.Exp).then_inc(prob_ready, 1)

            act.wait_ge(dve_consts, 1)
            schedule(act, body)

        @block.vector
        def _(dve):
            dve.wait_ge(consts_loaded, 16 * CONSTS)
            steps = [0]

            def const(instruction):
                steps[0] += 1
                instruction.then_inc(dve_step, 1)
                dve.wait_ge(dve_step, steps[0])

            const(nc.vector.memset(bias_p[:, :], 0.0))
            const(nc.vector.tensor_copy(bias_p[0:1, :], bias))
            const(nc.vector.tensor_tensor(bias_rest, bias, bias_p[0:1, :], ALU.subtract))
            part1 = parts[0:1, 0, 0:2, :].rearrange("p a n -> p (a n)")
            const(nc.vector.tensor_copy(part1, bias_rest))
            const(nc.vector.tensor_copy(bias_p[32:33, :], part1))
            const(nc.vector.tensor_tensor(bias, bias_rest, part1, ALU.subtract))
            const(nc.vector.tensor_copy(bias_p[64:65, :], bias))
            const(nc.vector.scalar_tensor_tensor(qk_scale[:, :], qn_col[:, :], SCALE, kn_col[:, :],
                                                 ALU.mult, ALU.mult))
            const(nc.vector.tensor_scalar(one_minus_mu[:, :, :], mu_col[:, :, :], -1.0, 1.0, ALU.mult, ALU.add))
            for i in range(2):
                const(nc.vector.memset(k_st[i][STACK:ROWS, :, :], 1.0))
                const(nc.vector.memset(v_own[i][:, :, :, :], 1.0))
                const(nc.vector.memset(v_mix[i][:, :, :, :], 1.0))
                const(nc.vector.memset(v_mix[i][0:WINDOW, 0, :, :], 0.0))
                const(nc.vector.memset(bank_o[i][:, :], 0.0))
            nc.vector.memset(x2T[:, :, 0:1], 0.0).then_inc(dve_consts, 1)
            dve.wait_ge(dve_consts, 1)

            def aggregate(st, mv, s, stats, mv_ready):
                for t in range(TILES):
                    count = held(dve, s.after(TILES, t + 1))
                    dve.wait_ge(dve_consts, 1)
                    dve.wait_ge(stats, count)
                    nc.vector.bn_aggr(mv[:, t, :], st[:, t, :]).then_inc(mv_ready, 1)

            def normalise(xn, src, mv, rstd, ready):
                for t in range(TILES):
                    nc.vector.tensor_scalar(xn[:, t, :], src[:, t, :], mv[:, t, 0:1], rstd[:, t:t + 1],
                                            ALU.subtract, ALU.mult).then_inc(ready, 1)

            def clip(f, t):
                dve.wait_ge(qk_done, f.after(TILES, t + 1))
                if t == 0:
                    if past(count := f.after(TILES, 0)):
                        dve.wait_ge(qkT_done, count)
                nc.vector.tensor_scalar(qk[:, t, :], bank_p[0][:, :], -CLIP, CLIP, ALU.max, ALU.min)\
                    .then_inc(qk_clipped, 1)

            def sum_squares(f, t):
                dve.wait_ge(sq_ready, f.after(TILES, t + 1))
                if t == 0:
                    if past(count := f.after(1, 0)):
                        dve.wait_ge(rms_ready, count)
                nc.vector.tensor_reduce(rms_v[:, 2 * HEADS * t:2 * HEADS * (t + 1)],
                                        sq[t % 2][:, :].rearrange("p (h d) -> p h d", d=HD),
                                        AX.X, ALU.add).then_inc(sumsq_ready, 1)

            def maximum(s, n):
                t, c = n // 4, n % 4
                dve.wait_ge(a_done, s.after(BANKS, n + 1))
                if n == 0:
                    if past(count := s.after(1, 0)):
                        dve.wait_ge(maxT_done, count)
                nc.vector.tensor_reduce(smax[:, t, 4 * c:4 * c + 4],
                                        bank_s[n % 2][:, :].rearrange("p (h k) -> p h k", h=4),
                                        AX.X, ALU.max).then_inc(max_ready, 1)

            def mix(g, c):
                which, k = c // KT, c % KT
                xm = (xr, xk)[which][:, k, :]
                dve.wait_ge(mixa_ready, g.after(2 * KT, c + 1))
                nc.vector.scalar_tensor_tensor(xm, x2T[:, k, 1:L + 1], mu_col[:, which, k:k + 1], xm,
                                               ALU.mult, ALU.add).then_inc(mixed, 1)

            def attended(s, t):
                dve.wait_ge(pv_done, s.after(BANKS, 4 * t + 4))
                if past(count := s.after(2 * TILES, 2 * t)):
                    dve.wait_ge(o_normed, count)
                nc.vector.transpose(o_tok[:, :, :].rearrange("p c r -> p (c r)"), bank_o[t % 2][:, :])\
                    .then_inc(o_turned, 1)
                dve.wait_ge(o_turned, s.after(TILES, t + 1))
                nc.vector.reciprocal(o_inv[:, :], o_tok[:, :, HD]).then_inc(o_inverse, 1)
                dve.wait_ge(o_inverse, s.after(TILES, t + 1))
                if past(count := s.after(TILES, t)):
                    dve.wait_ge(oT_ready, count)
                tok = o_tok[:, :, :].rearrange("p (k o b) r -> p k o b r", k=KT, o=2)
                inv = o_inv[:, :].rearrange("p (k o b x) -> p k o b x", k=KT, o=2, x=1)
                for odd in range(2):
                    nc.vector.tensor_tensor(
                        o_nrm[:, :, :, HD * odd:HD * odd + HD], tok[:, :, odd, :, 0:HD],
                        inv[:, :, odd, :, :].broadcast_to([P, KT, 4, HD]), ALU.mult).then_inc(o_normed, 1)
                dve.wait_ge(o_normed, s.after(2 * TILES, 2 * t + 2))
                if t == 0:
                    if past(count := s.after(TILES, 0)):
                        dve.wait_ge(wo_done, count)
                nc.vector.transpose(oT[:, t, :, :].rearrange("p b n -> p (b n)"),
                                    o_nrm[:, :, :, :].rearrange("p k b r -> p (k b r)")).then_inc(oT_ready, 1)

            def residual(s, t, bank):
                dve.wait_ge(wo_done, s.after(TILES, t + 1))
                if t == 0:
                    dve.wait_ge(res_loaded, s.after(16, 16))
                xt = x1[s.parity][:, t, :]
                nc.vector.tensor_tensor(xt, xt, bank[:, 0:D], ALU.add).then_inc(x1_ready, 1)

            def residual_stats(s, t):
                dve.wait_ge(x1_ready, s.after(TILES, t + 1))
                if t == 0:
                    if past(count := s.after(TILES, 0)):
                        dve.wait_ge(ln2_mv, count)
                nc.vector.bn_stats(st2[:, t, :], x1[s.parity][:, t, :]).then_inc(ln2_stats, 1)

            def body(s, lead, front, attend, ffn):
                e, f, g = s.shifted(2), s.shifted(1), s.shifted(-1)
                if front:
                    clip(f, 0)
                if ffn:
                    dve.wait_ge(ln2_rstd, g.after(1, 1))
                    if past(count := g.after(KT, 0)):
                        dve.wait_ge(x2T_done, count)
                    normalise(xn2, x1[g.parity], mv2, rstd2, xn2_ready)
                if front:
                    sum_squares(f, 0)
                for n in range(BANKS):
                    if attend:
                        maximum(s, n)
                    if front and n in (2, 7, 12):
                        clip(f, (2, 7, 12).index(n) + 1)
                    if front and n in (6, 11, 15):
                        sum_squares(f, (6, 11, 15).index(n) + 1)
                    if ffn and n in (3, 5, 8, 10):
                        mix(g, (3, 5, 8, 10).index(n))
                if front:
                    dve.wait_ge(rms_step, f.after(RMS_STEPS, 2))
                    if past(count := f.after(TILES, 0)):
                        dve.wait_ge(qkn_ready, count)
                    nc.vector.tensor_scalar(rms_r[:, :].bitcast(mybir.dt.int32), rms_v[:, :].bitcast(mybir.dt.int32),
                                            -0.5, float(0x5F3759DF), ALU.mult, ALU.add).then_inc(rms_seed, 1)
                if attend:
                    dve.wait_ge(maxT_done, s.after(1, 1))
                    dve.wait_ge(neg0_ready, s.after(1, 1))
                    if past(count := s.after(1, 0)):
                        dve.wait_ge(neg2_ready, count)
                    nc.vector.scalar_tensor_tensor(neg_rest[:, :], bank_t[0][0:HEADS, :], -1.0, neg_p[0][:, :],
                                                   ALU.mult, ALU.subtract).then_inc(neg_rest_ready, 1)
                if front:
                    for t in range(TILES):
                        if t == 0:
                            dve.wait_ge(rms_ready, f.after(1, 1))
                            dve.wait_ge(sq_ready, f.after(TILES, TILES))
                        q4 = qk[:, t, :].rearrange("p (h d) -> p h d", d=HD)
                        r4 = rms_r[:, 2 * HEADS * t:2 * HEADS * (t + 1)].rearrange("p (h o) -> p h o", o=1)
                        nc.vector.tensor_tensor(q4, q4, r4.broadcast_to([P, 2 * HEADS, HD]), ALU.mult)\
                            .then_inc(qkn_ready, 1)
                    for t in range(TILES):
                        dve.wait_ge(part0_ready, f.after(TILES, t + 1))
                        if past(count := f.after(TILES, t - 1)):
                            dve.wait_ge(part2_ready, count)
                        b4 = bank_t[t % 2][:, :].rearrange("p (b n) -> p b n", b=4)
                        cols = slice(P * t, P * t + P)
                        nc.vector.scalar_tensor_tensor(rest[t % 2][:, 0:2, :], b4[:, 0:2, :], qk_scale[:, :],
                                                       parts[:, 0:2, 0, cols], ALU.mult, ALU.subtract)
                        nc.vector.tensor_tensor(rest[t % 2][:, 2:4, :], b4[:, 2:4, :], parts[:, 2:4, 0, cols],
                                                ALU.subtract).then_inc(rest_ready, 1)
                for t in range(TILES):
                    if attend:
                        attended(s, t)
                        if t:
                            residual(s, t - 1, bank_p[(t - 1) % 2])
                            if t > 1:
                                residual_stats(s, t - 2)
                    if lead and t == 1:
                        dve.wait_ge(x_loaded, e.after(16, 16))
                        for i in range(TILES):
                            nc.vector.bn_stats(st1[:, i, :], x_in[:, i, :]).then_inc(ln1_stats, 1)
                        aggregate(st1, mv1, e, ln1_stats, ln1_mv)
                    if lead and t == 2:
                        dve.wait_ge(ln1_rstd, e.after(1, 1))
                        if past(count := e.after(KT, 0)):
                            dve.wait_ge(xT_done, count)
                        normalise(xn1, x_in, mv1, rstd1, xn1_ready)
                if ffn:
                    for t in range(TILES):
                        dve.wait_ge(kv_done, g.after(TILES, t + 1))
                        dve.wait_ge(gate_ready, g.after(TILES, t + 1))
                        nc.vector.scalar_tensor_tensor(gate[:, t, :], gate[:, t, :], 1.0,
                                                       bank_p[(t + 1) % 2][:, 0:D], ALU.add, ALU.mult)\
                            .then_inc(kvr_ready, 1)
                        if t == 0:
                            if attend:
                                residual_stats(s, TILES - 2)
                            dve.wait_ge(xn2_ready, g.after(TILES, TILES))
                        dve.wait_ge(kvr_ready, g.after(TILES, t + 1))
                        xt = x1[g.parity][:, t, :]
                        nc.vector.scalar_tensor_tensor(xt, gate[:, t, :], 0.5, xt, ALU.mult, ALU.add)\
                            .then_inc(y_ready, 1)
                if attend:
                    if not ffn:
                        residual_stats(s, TILES - 2)
                    if past(count := s.after(1, 0)):
                        dve.wait_ge(ln2_rstd, count)
                    if past(count := s.after(TILES, 0)):
                        dve.wait_ge(xn2_ready, count)
                    residual(s, TILES - 1, bank_p[1])
                    residual_stats(s, TILES - 1)
                    aggregate(st2, mv2, s, ln2_stats, ln2_mv)

            schedule(dve, body)

        @block.tensor
        def _(pe):
            pe.wait_ge(pool_consts, 1)
            pe.wait_ge(dve_consts, 1)
            pe.wait_ge(consts_loaded, 16 * CONSTS)

            def add_bias(dst, lo, n):
                nc.tensor.matmul(dst, ones_rows[:, :], bias_p[:, lo:lo + n], start=True, stop=False)

            def transposes(xn, done):
                for k in range(KT):
                    for t in range(TILES):
                        last = nc.tensor.transpose(bank_t[k][:, P * t:P * t + P], xn[:, t, P * k:P * k + P],
                                                   ident[:, :])
                    last.then_inc(done, 1)

            def token_product(dst, lhs, w, first, done):
                for k in range(KT):
                    last = nc.tensor.matmul(dst, lhs(k), w[:, k, :], start=(first and k == 0), stop=(k == KT - 1))
                last.then_inc(done, 1)

            def project_qk(s, f, t):
                if past(count := f.after(TILES, t)):
                    pe.wait_ge(qk_clipped, count)
                if t == 0:
                    if past(count := s.after(TILES, 0)):
                        pe.wait_ge(x1_ready, count)
                    if past(count := s.after(TILES, -TILES)):
                        pe.wait_ge(kvr_ready, count)
                    pe.wait_ge(xT_ready, f.after(KT, KT))
                add_bias(bank_p[0][:, :], 0, 2 * D)
                token_product(bank_p[0][:, :], lambda k: xT[:, k, P * t:P * t + P], w_qk, False, qk_done)

            def project_v(f, t):
                if past(count := f.after(TILES, t)):
                    pe.wait_ge(v_ready, count)
                add_bias(bank_p[1][:, 0:D], 2 * D, D)
                token_product(bank_p[1][:, 0:D], lambda k: xT[:, k, P * t:P * t + P], w_v, False, v_done)

            def scores_a(s, n):
                q, k = q_st[s.parity], k_st[s.parity]
                t, c = n // 4, n % 4
                dst = bank_s[n % 2]
                if n < 2:
                    if past(count := s.after(BANKS, 0)):
                        pe.wait_ge(prob_ready, count)
                else:
                    pe.wait_ge(max_ready, s.after(BANKS, n - 1))
                nc.tensor.matmul(dst[:, :], ident_b[:, :],
                                 mask_a[min(t, 1)][:, :, :].rearrange("p h k -> p (h k)"),
                                 start=True, stop=False, skip_group_check=True)
                for j in range(4):
                    for half in range(2):
                        h, i = 4 * c + j, 2 * t + half
                        lo = max(0, WINDOW * (i - 1))
                        hi = WINDOW * (i + 1)
                        last = nc.tensor.matmul(
                            dst[WINDOW * half:WINDOW * half + WINDOW, P * (j + 1) - (hi - lo):P * (j + 1)],
                            q[0:STACK, h, WINDOW * i:hi], k[0:STACK, h, lo:hi],
                            start=False, stop=True, skip_group_check=True)
                last.then_inc(a_done, 1)

            def scores_b(s, n):
                q, k = q_st[s.parity], k_st[s.parity]
                i, c = n // 2, n % 2
                dst = bank_s[n % 2]
                if n < 2:
                    pe.wait_ge(max_ready, s.after(BANKS, BANKS))
                else:
                    pe.wait_ge(prob_ready, s.after(BANKS, n - 1))
                nc.tensor.matmul(dst[:, :], ident_b[:, :],
                                 mask_b[min(i, 1)][:, :, :].rearrange("p h q -> p (h q)"),
                                 start=True, stop=False, skip_group_check=True)
                for j in range(8):
                    h = 8 * c + j
                    lo, hi = max(0, WINDOW * (i - 1)), WINDOW * (i + 1)
                    last = nc.tensor.matmul(dst[P - (hi - lo):P, WINDOW * j:WINDOW * j + WINDOW],
                                            k[0:ROWS, h, lo:hi], q[0:ROWS, h, WINDOW * i:hi],
                                            start=False, stop=True, skip_group_check=True)
                last.then_inc(b_done, 1)

            def times_v(s, n):
                i, c = n // 2, n % 2
                t = i // 2
                v = v_own[s.parity] if i % 2 else v_mix[s.parity]
                pe.wait_ge(prob_ready, s.after(BANKS, n + 1))
                if n % 4 == 0:
                    if past(count := s.after(TILES, t - 1)):
                        pe.wait_ge(o_turned, count)
                for j in range(8):
                    h = 8 * c + j
                    quad, row = h // 4, 32 * (h % 4)
                    col = P * quad + WINDOW * (i % 2)
                    last = nc.tensor.matmul(bank_o[t % 2][row:row + HD + 1, col:col + WINDOW],
                                            v[:, t, h, :], prob[n % 3][:, j, :], start=True, stop=True,
                                            tile_position=(0, row))
                last.then_inc(pv_done, 1)

            def output_product(s, t, bank):
                pe.wait_ge(oT_ready, s.after(TILES, t + 1))
                add_bias(bank[:, 0:D], 3 * D, D)
                token_product(bank[:, 0:D], lambda k: oT[:, t, k, :], w_o, False, wo_done)

            def body(s, lead, front, attend, ffn):
                f, g = s.shifted(1), s.shifted(-1)
                if front:
                    pe.wait_ge(xn1_ready, f.after(TILES, TILES))
                    if past(count := f.after(TILES, 0)):
                        pe.wait_ge(part0_ready, count)
                        pe.wait_ge(rest_ready, count)
                    transposes(xn1, xT_done)
                    project_qk(s, f, 0)
                    project_v(f, 0)
                if ffn:
                    pe.wait_ge(xn2_ready, g.after(TILES, TILES))
                    if front:
                        pe.wait_ge(xT_ready, f.after(KT, KT))
                    else:
                        pe.wait_ge(part0_ready, s.after(TILES, TILES) if attend else g.after(TILES, TILES))
                        pe.wait_ge(rest_ready, s.after(TILES, TILES) if attend else g.after(TILES, TILES))
                    transposes(xn2, x2T_done)
                for n in range(BANKS):
                    if attend:
                        if n == 0:
                            pe.wait_ge(stack_loaded[s.parity], s.after_half(16 * 12, 16 * 12))
                        scores_a(s, n)
                    if front and n in (2, 7, 12):
                        project_qk(s, f, (2, 7, 12).index(n) + 1)
                    if front and n in (4, 9, 14):
                        project_v(f, (4, 9, 14).index(n) + 1)
                if ffn:
                    pe.wait_ge(mixed, g.after(2 * KT, 2 * KT))
                    pe.wait_ge(x2T_ready, g.after(KT, KT))
                    for m in range(KT):
                        for k in range(KT):
                            last = nc.tensor.matmul(bank_t[m][:, :], w_k[:, k, P * m:P * m + P], xk[:, k, :],
                                                    start=(k == 0), stop=(k == KT - 1))
                        last.then_inc(k_done, 1)
                if attend:
                    pe.wait_ge(max_ready, s.after(BANKS, BANKS))
                    if ffn:
                        pe.wait_ge(relu_ready, g.after(KT, 1))
                    elif front:
                        pe.wait_ge(xT_ready, f.after(KT, KT))
                    for t in range(TILES):
                        last = nc.tensor.transpose(bank_t[0][0:HEADS, P * t:P * t + P], smax[:, t, :], ident[:, :])
                    last.then_inc(maxT_done, 1)
                if ffn:
                    for t in range(TILES):
                        if t < 2:
                            if front:
                                pe.wait_ge(qk_clipped, f.after(TILES, TILES))
                                pe.wait_ge(v_ready, f.after(TILES, TILES))
                            else:
                                pe.wait_ge(x1_ready, g.after(TILES, TILES))
                                pe.wait_ge(kvr_ready, g.after(TILES, 0))
                        else:
                            pe.wait_ge(gate_ready, g.after(TILES, t - 1))
                        token_product(bank_p[t % 2][:, 0:D], lambda k: xr[:, k, P * t:P * t + P], w_r, True, r_done)
                if front:
                    for t in range(TILES):
                        pe.wait_ge(qkn_ready, f.after(TILES, t + 1))
                        if t == 0:
                            if attend:
                                pe.wait_ge(neg0_ready, s.after(1, 1))
                                pe.wait_ge(neg_rest_ready, s.after(1, 1))
                            if ffn:
                                pe.wait_ge(relu_ready, g.after(KT, KT))
                            pe.wait_ge(xT_ready, f.after(KT, KT))
                        elif t >= 2:
                            pe.wait_ge(part0_ready, f.after(TILES, t - 1))
                            pe.wait_ge(rest_ready, f.after(TILES, t - 1))
                        for b in range(4):
                            last = nc.tensor.transpose(bank_t[t % 2][:, P * b:P * b + P], qk[:, t, P * b:P * b + P],
                                                       ident[:, :])
                        last.then_inc(qkT_done, 1)
                if attend:
                    pe.wait_ge(max_rows_loaded, s.after(16 * PARTS, 16 * PARTS))
                    scores_b(s, 0)
                    for n in range(BANKS):
                        if n + 1 < BANKS:
                            scores_b(s, n + 1)
                        times_v(s, n)
                        if n % 4 == 3 and n > 4:
                            t = n // 4 - 1
                            if t < 2 and ffn:
                                pe.wait_ge(gate_ready, g.after(TILES, TILES))
                            elif t < 2 and front:
                                pe.wait_ge(qk_clipped, f.after(TILES, TILES))
                                pe.wait_ge(v_ready, f.after(TILES, TILES))
                            if t == 2:
                                pe.wait_ge(x1_ready, s.after(TILES, 1))
                            output_product(s, t, bank_p[t % 2])
                if ffn:
                    pe.wait_ge(kact_ready, g.after(KT, KT))
                    for t in range(TILES):
                        if t < 2:
                            if attend:
                                pe.wait_ge(x1_ready, s.after(TILES, t + 2))
                            else:
                                pe.wait_ge(gate_ready, g.after(TILES, TILES))
                        else:
                            pe.wait_ge(kvr_ready, g.after(TILES, t - 1))
                        token_product(bank_p[(t + 1) % 2][:, 0:D], lambda k: kact[:, k, P * t:P * t + P], w_f,
                                      True, kv_done)
                if attend:
                    if ffn:
                        pe.wait_ge(kvr_ready, g.after(TILES, 3))
                    else:
                        pe.wait_ge(x1_ready, s.after(TILES, 2))
                    output_product(s, TILES - 1, bank_p[1])

            schedule(pe, body)


def kernel(L0_attn_x, L0_attn_wq_w, L0_attn_wq_b, L0_attn_wk_w, L0_attn_wk_b, L0_attn_wv_w, L0_attn_wv_b,
           L0_attn_wo_w, L0_attn_wo_b, L0_attn_qn_w, L0_attn_kn_w, L0_ffn_W_r, L0_ffn_W_k, L0_ffn_W_v,
           L0_ffn_mu_r, L0_ffn_mu_k):
    import concourse.bacc as bacc
    from concourse.bass_utils import run_bass_kernel_spmd

    wo = np.asarray(L0_attn_wo_w).T.reshape(KT, 2, 4, HD, D).transpose(0, 2, 1, 3, 4)
    arrays = {
        "x": np.asarray(L0_attn_x).reshape(SEQS * L, D),
        "wqkT": np.concatenate([np.asarray(L0_attn_wq_w).T, np.asarray(L0_attn_wk_w).T], axis=1),
        "wvT": np.asarray(L0_attn_wv_w).T,
        "woP": wo.reshape(D, D),
        "wrT": np.asarray(L0_ffn_W_r).T,
        "wkT": np.asarray(L0_ffn_W_k).T,
        "wfT": np.asarray(L0_ffn_W_v).T,
        "bqkv": np.concatenate([np.asarray(L0_attn_wq_b), np.asarray(L0_attn_wk_b),
                                np.asarray(L0_attn_wv_b)]).reshape(1, 3 * D),
        "bo": np.asarray(L0_attn_wo_b).reshape(1, D),
        "qn": np.tile(np.asarray(L0_attn_qn_w), P // HD).reshape(P, 1),
        "kn": np.tile(np.asarray(L0_attn_kn_w), P // HD).reshape(P, 1),
        "mu": np.stack([np.asarray(L0_ffn_mu_r).reshape(KT, P), np.asarray(L0_ffn_mu_k).reshape(KT, P)])
        .transpose(2, 0, 1),
    }
    arrays = {k: np.ascontiguousarray(v) for k, v in arrays.items()}
    nc = bacc.Bacc("TRN2", target_bir_lowering=False, num_devices=1)
    ins = [nc.dram_tensor(k, v.shape, FP32, kind="ExternalInput").ap() for k, v in arrays.items()]
    out = nc.dram_tensor("out", (SEQS * L, D), FP32, kind="ExternalOutput").ap()
    build(nc, *ins, out)
    r = run_bass_kernel_spmd(nc, [arrays], core_ids=[0])
    return r.results[0]["out"].reshape(SEQS, L, D)
```

```python
from contextlib import ExitStack

import numpy as np
import concourse.bass as bass
from concourse import mybir

FP32 = mybir.dt.float32
FP32R = mybir.dt.float32r
BF16 = mybir.dt.bfloat16
INT32 = mybir.dt.int32
ALU = mybir.AluOpType
ACT = mybir.ActivationFunctionType
AX = mybir.AxisListType

SEQS, L, D = 32, 512, 256
HEADS, HD = 16, 16
WINDOW = 64
P = 128
TILES = L // P
KT = D // P
BLOCKS = L // WINDOW
PARTS = 3
Q_SLOTS = (0, 0, 0, 1, 1, 2)
K_SLOTS = (0, 1, 2, 0, 1, 0)
GROUP = P // HD
STACK = HD * len(Q_SLOTS)
ROWS = STACK + PARTS
LN_EPS = 1e-5
RMS_EPS = 1e-5
CLIP = 1e4
SCALE = float(HD) ** -0.5
MASKED = -1e30
ONES_PAIR = 0x3F803F80


class Seq:

    def __init__(self, pair, offset):
        self.pair, self.offset = pair, offset
        self.n = 2 * pair + offset
        self.parity = offset % 2
        self.half = pair + offset // 2

    def shifted(self, by):
        return Seq(self.pair, self.offset + by)

    def after(self, per, k):
        return self.n * per + k

    def after_half(self, per, k):
        return self.half * per + k


def past(count):
    return not isinstance(count, int) or count > 0


def held(eng, count):
    return count if isinstance(count, int) else eng.to_reg(count)


def build(nc, x, wqkT, wvT, woP, wrT, wkT, wfT, bqk, bo, bv, qn, kn, mu, out):
    ctx = ExitStack()
    with ctx:
        def sb(name, shape, dt=FP32):
            return ctx.enter_context(nc.sbuf_tensor(name, shape, dt))

        def ps(name):
            return ctx.enter_context(nc.psum_tensor(name, [P, 512], FP32))

        def sem(name):
            return ctx.enter_context(nc.semaphore(name))

        w_qk_hi = sb("w_qk_hi", [P, KT, 2 * D], FP32R)
        w_qk_lo = sb("w_qk_lo", [P, KT, 2 * D], FP32R)
        w_k_hi = sb("w_k_hi", [P, KT, D], FP32R)
        w_k_lo = sb("w_k_lo", [P, KT, D], FP32R)
        w_v = sb("w_v", [P, KT, D])
        w_o = sb("w_o", [P, KT, D])
        w_r = sb("w_r", [P, KT, D])
        w_f = sb("w_f", [P, KT, D])
        bias_p = sb("bias_p", [65, 3 * D], BF16)
        ones_rows = sb("ones_rows", [65, P], BF16)
        bv_col = sb("bv_col", [P, KT])
        bo_all = sb("bo_all", [P, D])
        qn_col = sb("qn_col", [P, 1])
        kn_col = sb("kn_col", [P, 1])
        qk_scale = sb("qk_scale", [P, 1])
        mu_col = sb("mu_col", [P, 2, KT])
        one_minus_mu = sb("one_minus_mu", [P, 2, KT])
        minus_half = sb("minus_half", [P, TILES])
        ident = sb("ident", [P, P])
        ident_b = sb("ident_b", [P, P], BF16)
        mask_a = [sb(f"mask_a{i}", [P, 4, P], BF16) for i in range(2)]
        mask_b = [sb(f"mask_b{i}", [P, 8, WINDOW], BF16) for i in range(2)]

        x_in = sb("x_in", [P, TILES, D])
        xT = sb("xT", [P, KT, L])
        xT_hi = sb("xT_hi", [P, KT, L], FP32R)
        xT_lo = sb("xT_lo", [P, KT, L], FP32R)
        qk = sb("qk", [P, TILES, 2 * D])
        bias = qk[0:1, 0:2, :].rearrange("p a n -> p (a n)")[:, 0:3 * D]
        bias_rest = qk[0:1, 2:4, :].rearrange("p a n -> p (a n)")[:, 0:3 * D]
        sq = [sb(f"sq{i}", [P, 2 * D]) for i in range(2)]
        rms_v = sb("rms_v", [P, TILES * 2 * HEADS])
        rms_r = sb("rms_r", [P, TILES * 2 * HEADS])
        rms_w = sb("rms_w", [P, TILES * 2 * HEADS])
        parts = sb("parts", [P, 4, PARTS, L], BF16)
        rest = [sb(f"rest{i}", [P, 4, P]) for i in range(2)]
        q_st = [sb(f"q_st{i}", [P, HEADS, L], BF16) for i in range(2)]
        k_st = [sb(f"k_st{i}", [P, HEADS, L], BF16) for i in range(2)]
        v_own = [sb(f"v_own{i}", [P, TILES, HEADS, HD + 1]) for i in range(2)]
        v_mix = [sb(f"v_mix{i}", [P, TILES, HEADS, HD + 1]) for i in range(2)]
        smax = sb("smax", [P, TILES, HEADS])
        neg_rest = sb("neg_rest", [HEADS, L])
        neg_p = [sb(f"neg_p{i}", [HEADS, L], BF16) for i in range(PARTS)]
        prob = [sb(f"prob{i}", [P, 8, WINDOW]) for i in range(3)]
        o_tok = sb("o_tok", [P, 16, 32])
        o_inv = sb("o_inv", [P, 16])
        o_nrm = sb("o_nrm", [P, KT, 4, 32])
        oT = sb("oT", [P, TILES, KT, P])
        x1 = [sb(f"x1_{i}", [P, TILES, D]) for i in range(2)]
        x2T = sb("x2T", [P, KT, L + 1])
        xr = sb("xr", [P, KT, L])
        xk_hi = sb("xk_hi", [P, KT, L], FP32R)
        xk_lo = sb("xk_lo", [P, KT, L], FP32R)
        x2_mu = [r[:, :, :].rearrange("p b n -> p (b n)") for r in rest]
        kact = sb("kact", [P, KT, L])
        xn2 = kact[:, :, :].rearrange("p k (a d) -> p (k a) d", d=D)
        gate = sb("gate", [P, TILES, D])
        xk = gate[:, :, :].rearrange("p (k a) d -> p k (a d)", k=KT)
        w_qk, w_k = xT, xr[:, :, 0:D]
        st1 = sb("st1", [P, TILES, 6])
        mv1 = sb("mv1", [P, TILES, 2])
        rstd1 = sb("rstd1", [P, TILES])
        st2 = sb("st2", [P, TILES, 6])
        mv2 = sb("mv2", [P, TILES, 2])
        rstd2 = sb("rstd2", [P, TILES])

        bank_t = [ps(f"bank_t{i}") for i in range(2)]
        bank_p = [ps(f"bank_p{i}") for i in range(2)]
        bank_s = [ps(f"bank_s{i}") for i in range(2)]
        bank_o = [ps(f"bank_o{i}") for i in range(2)]
        bank_a = bank_s + bank_o

        def sems(*names):
            return [sem(n) for n in names]

        consts_loaded, x_loaded, res_loaded, y_stored, max_rows_loaded = sems(
            "consts_loaded", "x_loaded", "res_loaded", "y_stored", "max_rows_loaded")
        stack_loaded = [sem(f"stack_loaded{i}") for i in range(2)]
        pool_consts, pool_step, ln1_eps, ln1_rstd, ln2_eps, ln2_rstd, part2_ready = sems(
            "pool_consts", "pool_step", "ln1_eps", "ln1_rstd", "ln2_eps", "ln2_rstd", "part2_ready")
        res_biased, y_ready, xT_lo_ready, xk_lo_ready = sems("res_biased", "y_ready", "xT_lo_ready", "xk_lo_ready")
        dve_consts, dve_step, ln1_stats, ln1_mv, xn1_ready, ln2_stats, ln2_mv, xn2_ready = sems(
            "dve_consts", "dve_step", "ln1_stats", "ln1_mv", "xn1_ready", "ln2_stats", "ln2_mv", "xn2_ready")
        qk_clipped, sumsq_ready, qkn_ready, rest_ready, max_ready, neg_rest_ready, neg2_ready = sems(
            "qk_clipped", "sumsq_ready", "qkn_ready", "rest_ready", "max_ready", "neg_rest_ready",
            "neg2_ready")
        rms_step, rms_ready, xT_hi_ready, xk_hi_ready = sems("rms_step", "rms_ready", "xT_hi_ready", "xk_hi_ready")
        bo_ready, mixed, kvr_ready, o_turned, o_inverse, o_normed, oT_ready, x1_ready = sems(
            "bo_ready", "mixed", "kvr_ready", "o_turned", "o_inverse", "o_normed", "oT_ready", "x1_ready")
        xT_ready, sq_ready, v_ready, part0_ready, part1_ready, neg0_ready, neg1_ready = sems(
            "xT_ready", "sq_ready", "v_ready", "part0_ready", "part1_ready", "neg0_ready", "neg1_ready")
        x2T_ready, halves_ready, relu_ready, kact_ready, gate_ready, prob_ready = sems(
            "x2T_ready", "halves_ready", "relu_ready", "kact_ready", "gate_ready", "prob_ready")
        xT_done, qk_done, v_done, qkT_done, a_done, maxT_done, b_done, pv_done, wo_done = sems(
            "xT_done", "qk_done", "v_done", "qkT_done", "a_done", "maxT_done", "b_done", "pv_done", "wo_done")
        bo_done, x2T_done, k_done, r_done, kv_done = sems("bo_done", "x2T_done", "k_done", "r_done", "kv_done")

        CONSTS = 12
        BANKS = TILES * HEADS // 4

        STACK_LOADS = 16 * 2 * len(Q_SLOTS)

        QK_AT, V_AT = (4, 10), (7, 13)
        SPLIT_AT = (1, 4, 7, 10)

        r_bank = (bank_p[0], bank_p[1], bank_o[0], bank_o[1])
        kv_bank = (bank_p[1], bank_p[0], bank_o[1], bank_p[1])

        NEWTON = 3
        RMS_STEPS = 3 + 3 * NEWTON - 1
        SEED = 0x5F3759DF - (1 << 22)

        def schedule(eng, body):
            body(Seq(0, -2), True, False, False, False)
            body(Seq(0, -1), True, True, False, False)
            body(Seq(0, 0), True, True, True, False)
            body(Seq(0, 1), True, True, True, True)
            with eng.Fori(0, (SEQS - 4) // 2) as pair:
                body(Seq(pair, 2), True, True, True, True)
                body(Seq(pair, 3), True, True, True, True)
            body(Seq(0, SEQS - 2), False, True, True, True)
            body(Seq(0, SEQS - 1), False, False, True, True)
            body(Seq(0, SEQS), False, False, False, True)

        block = ctx.enter_context(nc.Block())

        @block.sync
        def _(sp):
            for dst, src in ((w_qk, wqkT), (w_v, wvT), (w_r, wrT), (w_k, wkT), (w_f, wfT)):
                sp.dma_start(dst[:, :, :], src.rearrange("(k p) n -> p k n", p=P)).then_inc(consts_loaded, 16)
            sp.dma_start(w_o[:, :, :], woP.rearrange("(k p) n -> p k n", p=P)).then_inc(consts_loaded, 16)
            sp.dma_start(bias[:, 0:2 * D], bqk).then_inc(consts_loaded, 16)
            sp.dma_start(bias[:, 2 * D:3 * D], bo).then_inc(consts_loaded, 16)
            sp.dma_start(bv_col[:, :], bv).then_inc(consts_loaded, 16)
            sp.dma_start(qn_col[:, :], qn).then_inc(consts_loaded, 16)
            sp.dma_start(kn_col[:, :], kn).then_inc(consts_loaded, 16)
            sp.dma_start(mu_col[:, :, :], mu).then_inc(consts_loaded, 16)

            def rows(dram, s):
                return dram[bass.ds(s.n * L, L), :].rearrange("(t p) d -> p t d", p=P)

            def store(s):
                count = held(sp, s.after(TILES, TILES))
                sp.wait_ge(consts_loaded, 16 * CONSTS)
                sp.wait_ge(y_ready, count)
                sp.dma_start(rows(out, s), x1[s.parity][:, :, :]).then_inc(y_stored, 16)

            def body(s, lead, front, attend, ffn):
                e, f, g = s.shifted(2), s.shifted(1), s.shifted(-1)
                if lead:
                    if past(count := e.after(KT, 0)):
                        count = held(sp, count)
                        sp.wait_ge(consts_loaded, 16 * CONSTS)
                        sp.wait_ge(xT_done, count)
                    sp.dma_start(x_in[:, :, :], rows(x, e)).then_inc(x_loaded, 16)
                if past(s.after(1, -1)):
                    store(s.shifted(-2))
                if attend:
                    if past(count := g.after(16, 0)):
                        count = held(sp, count)
                        sp.wait_ge(consts_loaded, 16 * CONSTS)
                        sp.wait_ge(y_stored, count)
                    sp.dma_start(x1[s.parity][:, :, :], rows(x, s)).then_inc(res_loaded, 16)
                if attend:
                    for i, ready in enumerate((neg0_ready, neg1_ready, neg2_ready)):
                        count = held(sp, s.after(1, 1))
                        sp.wait_ge(consts_loaded, 16 * CONSTS)
                        sp.wait_ge(ready, count)
                        sp.dma_start(q_st[s.parity][STACK + i:STACK + i + 1, :, :], neg_p[i][:, :])\
                            .then_inc(max_rows_loaded, 16)
                if front:
                    if past(count := f.after(BANKS, -BANKS)):
                        count = held(sp, count)
                        sp.wait_ge(consts_loaded, 16 * CONSTS)
                        sp.wait_ge(b_done, count)
                    for part, ready in enumerate((part0_ready, part1_ready, part2_ready)):
                        count = held(sp, f.after(TILES, TILES))
                        sp.wait_ge(consts_loaded, 16 * CONSTS)
                        sp.wait_ge(ready, count)
                        for st, which, slots in ((q_st, 0, Q_SLOTS), (k_st, 1, K_SLOTS)):
                            for slot in range(len(slots)):
                                if slots[slot] == part:
                                    sp.dma_start(st[f.parity][HD * slot:HD * slot + HD, :, :],
                                                 parts[:, KT * which:KT * which + KT, part, :])\
                                        .then_inc(stack_loaded[f.parity], 16)

            schedule(sp, body)
            store(Seq(0, SEQS - 1))
            sp.wait_ge(y_stored, 16 * SEQS)

        @block.gpsimd
        def _(pool):
            steps = [0]

            def const(instruction):
                steps[0] += 1
                instruction.then_inc(pool_step, 1)
                pool.wait_ge(pool_step, steps[0])

            def fill_mask(m, rows, pattern, base, per_row):
                view = m[rows[0]:rows[1], :, :]
                const(nc.gpsimd.affine_select(out=view, in_=view, compare_op=ALU.is_ge, fill=MASKED,
                                              base=base, pattern=pattern, channel_multiplier=per_row))

            for m in (ident, ident_b):
                const(nc.gpsimd.memset(m[:, :], 0.0))
                const(nc.gpsimd.affine_select(out=m[:, :], in_=m[:, :], compare_op=ALU.not_equal, fill=1.0,
                                              base=0, pattern=[[-1, P]], channel_multiplier=1))
            for m in (*mask_a, *mask_b):
                const(nc.gpsimd.memset(m[:, :, :], 0.0))
            W = WINDOW
            for i, m in enumerate(mask_a):
                for half in range(2):
                    rows = (W * half, W * half + W)
                    fill_mask(m, rows, [[0, 4], [1, P]], -1, -1)
                    fill_mask(m, rows, [[0, 4], [-1, P]], W, 1)
                if i == 0:
                    fill_mask(m, (0, W), [[0, 4], [1, P]], -W, 0)
            for m in mask_b:
                fill_mask(m, (0, P), [[0, 8], [-1, W]], -1, 1)
                fill_mask(m, (0, P), [[0, 8], [1, W]], W, -1)
            fill_mask(mask_b[0], (0, W), [[0, 8], [0, W]], -1, 0)
            const(nc.gpsimd.memset(minus_half[:, :], -0.5))
            nc.gpsimd.memset(ones_rows[:, :], 1.0).then_inc(pool_consts, 1)

            def mix(g, c):
                which, k = 1 - c // KT, c % KT
                xm = (xr, xk)[which][:, k, :]
                pool.wait_ge(halves_ready, g.after(2 * KT, c + 1))
                nc.gpsimd.tensor_tensor(xm, xm, x2_mu[c % 2], ALU.add).then_inc(mixed, 1)

            def less_high_xk(g, k):
                pool.wait_ge(xk_hi_ready, g.after(KT, k + 1))
                nc.gpsimd.tensor_tensor(xk_lo[:, k, :], xk[:, k, :], xk_hi[:, k, :].bitcast(FP32),
                                        ALU.subtract).then_inc(xk_lo_ready, 1)

            def output(g, t):
                pool.wait_ge(kvr_ready, g.after(TILES, t + 1))
                xt = x1[g.parity][:, t, :]
                nc.gpsimd.tensor_tensor(xt, xt, gate[:, t, :], ALU.add).then_inc(y_ready, 1)

            def body(s, lead, front, attend, ffn):
                e, f, g = s.shifted(2), s.shifted(1), s.shifted(-1)
                if ffn:
                    mix(g, 0)
                    mix(g, 1)
                    mix(g, 2)
                    less_high_xk(g, 0)
                    mix(g, 3)
                    less_high_xk(g, 1)
                if attend:
                    pool.wait_ge(res_loaded, s.after(16, 16))
                    nc.gpsimd.tensor_tensor(
                        x1[s.parity][:, :, :], x1[s.parity][:, :, :],
                        bo_all[:, :].rearrange("p (o d) -> p o d", o=1).broadcast_to([P, TILES, D]), ALU.add)\
                        .then_inc(res_biased, 1)
                if lead:
                    count = held(pool, e.after(TILES, TILES))
                    pool.wait_ge(dve_consts, 1)
                    pool.wait_ge(ln1_mv, count)
                    nc.gpsimd.tensor_scalar(rstd1[:, :], mv1[:, :, 1], LN_EPS, None, ALU.add).then_inc(ln1_eps, 1)
                    pool.wait_ge(ln1_eps, e.after(1, 1))
                    nc.gpsimd.tensor_tensor(rstd1[:, :], rstd1[:, :], minus_half[:, :], ALU.pow).then_inc(ln1_rstd, 1)
                if lead:
                    for t in range(TILES):
                        if t == 0:
                            count = held(pool, e.after(1, 1))
                            pool.wait_ge(dve_consts, 1)
                            pool.wait_ge(ln1_rstd, count)
                        nc.gpsimd.tensor_scalar(x_in[:, t, :], x_in[:, t, :], mv1[:, t, 0:1], rstd1[:, t:t + 1],
                                                ALU.subtract, ALU.mult).then_inc(xn1_ready, 1)
                if front:
                    for t in range(TILES):
                        if t == 0:
                            if past(count := s.after_half(STACK_LOADS, STACK_LOADS)):
                                pool.wait_ge(stack_loaded[s.parity], count)
                        pool.wait_ge(rest_ready, f.after(TILES, t + 1))
                        pool.wait_ge(part1_ready, f.after(TILES, t + 1))
                        nc.gpsimd.tensor_tensor(parts[:, :, 2, P * t:P * t + P], rest[t % 2][:, :, :],
                                                parts[:, :, 1, P * t:P * t + P], ALU.subtract)\
                            .then_inc(part2_ready, 1)

                if lead:
                    for k in range(KT):
                        pool.wait_ge(xT_hi_ready, e.after(KT, k + 1))
                        nc.gpsimd.tensor_tensor(xT_lo[:, k, :], xT[:, k, :], xT_hi[:, k, :].bitcast(FP32), ALU.subtract)\
                            .then_inc(xT_lo_ready, 1)
                if attend:
                    count = held(pool, s.after(TILES, TILES))
                    pool.wait_ge(dve_consts, 1)
                    pool.wait_ge(ln2_mv, count)
                    nc.gpsimd.tensor_scalar(rstd2[:, :], mv2[:, :, 1], LN_EPS, None, ALU.add).then_inc(ln2_eps, 1)
                    pool.wait_ge(ln2_eps, s.after(1, 1))
                    nc.gpsimd.tensor_tensor(rstd2[:, :], rstd2[:, :], minus_half[:, :], ALU.pow).then_inc(ln2_rstd, 1)
                if ffn:
                    for t in range(TILES):
                        output(g, t)

            pool.wait_ge(bo_ready, 1)
            schedule(pool, body)

        @block.scalar
        def _(act):
            def copy_v(f, t):
                act.wait_ge(v_done, f.after(TILES, t + 1))
                if t == 0:
                    if past(count := f.after(BANKS, -BANKS)):
                        act.wait_ge(pv_done, count)
                v4 = bank_p[1][:, 0:D].rearrange("p (h d) -> p h d", d=HD)
                own, mix = v_own[f.parity], v_mix[f.parity]
                nc.scalar.activation(own[:, t, :, 0:HD], v4, ACT.Copy)
                last = nc.scalar.activation(mix[WINDOW:P, t, :, 0:HD], v4[0:WINDOW], ACT.Copy)
                if t + 1 < TILES:
                    last = nc.scalar.activation(mix[0:WINDOW, t + 1, :, 0:HD], v4[WINDOW:P], ACT.Copy)
                last.then_inc(v_ready, 1)

            def squares(f, t):
                act.wait_ge(qk_clipped, f.after(TILES, t + 1))
                if past(count := f.after(TILES, t - 1)):
                    act.wait_ge(sumsq_ready, count)
                nc.scalar.activation(sq[t % 2][:, :], qk[:, t, :], ACT.Square).then_inc(sq_ready, 1)

            def v_and_squares(f, t):
                copy_v(f, t)
                squares(f, t)

            def halves(s, g, c, attend):
                which, k = 1 - c // KT, c % KT
                act.wait_ge(x2T_ready, g.after(KT, KT))
                if c == KT:
                    if past(count := g.after(TILES, 0)):
                        act.wait_ge(r_done, count)
                if c == 0:
                    if past(count := g.after(TILES, 0)):
                        act.wait_ge(y_ready, count)
                nc.scalar.activation((xr, xk)[which][:, k, :], x2T[:, k, 0:L], ACT.Copy,
                                     scale=one_minus_mu[:, which, k:k + 1])
                if c == 0:
                    act.wait_ge(part2_ready, (s if attend else g).after(TILES, TILES))
                if past(count := g.after(2 * KT, c - 1)):
                    act.wait_ge(mixed, count)
                nc.scalar.activation(x2_mu[c % 2], x2T[:, k, 1:L + 1], ACT.Copy,
                                     scale=mu_col[:, which, k:k + 1]).then_inc(halves_ready, 1)

            def tanh_r(g, t):
                act.wait_ge(r_done, g.after(TILES, t + 1))
                if t == 0:
                    if past(count := g.after(TILES, 0)):
                        act.wait_ge(y_ready, count)
                nc.scalar.activation(gate[:, t, :], r_bank[t][:, 0:D], ACT.Tanh, scale=0.5)\
                    .then_inc(gate_ready, 1)

            def part_0(s, f, t):
                act.wait_ge(qkT_done, f.after(TILES, t + 1))
                if t == 0:
                    if past(count := s.after_half(STACK_LOADS, STACK_LOADS)):
                        act.wait_ge(stack_loaded[s.parity], count)
                b4 = bank_t[t % 2][:, :].rearrange("p (b n) -> p b n", b=4)
                cols = slice(P * t, P * t + P)
                nc.scalar.activation(parts[:, 0:2, 0, cols], b4[:, 0:2, :], ACT.Copy, scale=qk_scale[:, :])
                nc.scalar.activation(parts[:, 2:4, 0, cols], b4[:, 2:4, :], ACT.Copy).then_inc(part0_ready, 1)

            def part_1(f, t):
                act.wait_ge(rest_ready, f.after(TILES, t + 1))
                nc.scalar.activation(parts[:, :, 1, P * t:P * t + P], rest[t % 2][:, :, :], ACT.Copy)\
                    .then_inc(part1_ready, 1)

            def body(s, lead, front, attend, ffn):
                e, f, g = s.shifted(2), s.shifted(1), s.shifted(-1)
                if front:
                    v_and_squares(f, 0)
                if ffn:
                    for k in range(KT):
                        act.wait_ge(x2T_done, g.after(KT, k + 1))
                        if k == 0:
                            if past(count := g.after(2 * KT, 0)):
                                act.wait_ge(halves_ready, count)
                        nc.scalar.activation(x2T[:, k, 1:L + 1], bank_t[k][:, :], ACT.Copy).then_inc(x2T_ready, 1)
                    halves(s, g, 0, attend)
                    halves(s, g, 1, attend)
                if front:
                    v_and_squares(f, 1)
                if ffn:
                    halves(s, g, 2, attend)
                    halves(s, g, 3, attend)
                if front:
                    v_and_squares(f, 2)
                if attend:
                    act.wait_ge(maxT_done, s.after(1, 1))
                    if past(count := s.after(16 * PARTS, 0)):
                        act.wait_ge(max_rows_loaded, count)
                    nc.scalar.activation(neg_p[0][:, :], bank_s[0][0:HEADS, :], ACT.Copy, scale=-1.0)\
                        .then_inc(neg0_ready, 1)
                if front:
                    squares(f, TILES - 1)
                if attend:
                    act.wait_ge(neg_rest_ready, s.after(1, 1))
                    nc.scalar.activation(neg_p[1][:, :], neg_rest[:, :], ACT.Copy).then_inc(neg1_ready, 1)
                if front:
                    copy_v(f, TILES - 1)
                for m in range(KT):
                    if ffn:
                        act.wait_ge(k_done, g.after(KT, m + 1))
                        if m == 0:
                            if past(count := g.after(TILES, 0)):
                                act.wait_ge(kv_done, count)
                        nc.scalar.activation(kact[:, m, :], bank_t[m][:, :], ACT.Relu).then_inc(relu_ready, 1)
                        act.wait_ge(relu_ready, g.after(KT, m + 1))
                        nc.scalar.activation(kact[:, m, :], kact[:, m, :], ACT.Square).then_inc(kact_ready, 1)
                if ffn:
                    for t in range(TILES - 1):
                        tanh_r(g, t)
                for n in range(BANKS):
                    if attend:
                        act.wait_ge(b_done, s.after(BANKS, n + 1))
                        if past(count := s.after(BANKS, n - 2)):
                            act.wait_ge(pv_done, count)
                        nc.scalar.activation(prob[n % 3][:, :, :].rearrange("p h q -> p (h q)"), bank_s[n % 2][:, :],
                                             ACT.Exp).then_inc(prob_ready, 1)
                    if ffn and n == 0:
                        tanh_r(g, TILES - 1)
                    if front and n - 2 in SPLIT_AT:
                        part_1(f, SPLIT_AT.index(n - 2))
                    if front and n in SPLIT_AT:
                        part_0(s, f, SPLIT_AT.index(n))
                if lead:
                    for k in range(KT):
                        act.wait_ge(xT_done, e.after(KT, k + 1))
                        if k == 0:
                            if past(count := e.after(TILES, 0)):
                                act.wait_ge(v_done, count)
                        nc.scalar.activation(xT[:, k, :], bank_t[k][:, :], ACT.Copy).then_inc(xT_ready, 1)

            act.wait_ge(dve_consts, 1)
            schedule(act, body)

        @block.vector
        def _(dve):
            dve.wait_ge(consts_loaded, 16 * CONSTS)
            steps = [0]

            def const(instruction):
                steps[0] += 1
                instruction.then_inc(dve_step, 1)
                dve.wait_ge(dve_step, steps[0])

            const(nc.vector.memset(bias_p[:, :], 0.0))
            const(nc.vector.tensor_copy(bias_p[0:1, :], bias))
            const(nc.vector.tensor_tensor(bias_rest, bias, bias_p[0:1, :], ALU.subtract))
            part1 = parts[0:1, 0, 0:2, :].rearrange("p a n -> p (a n)")[:, 0:3 * D]
            const(nc.vector.tensor_copy(part1, bias_rest))
            const(nc.vector.tensor_copy(bias_p[32:33, :], part1))
            const(nc.vector.tensor_tensor(bias, bias_rest, part1, ALU.subtract))
            const(nc.vector.tensor_copy(bias_p[64:65, :], bias))
            const(nc.vector.scalar_tensor_tensor(qk_scale[:, :], qn_col[:, :], SCALE, kn_col[:, :],
                                                 ALU.mult, ALU.mult))
            const(nc.vector.tensor_scalar(one_minus_mu[:, :, :], mu_col[:, :, :], -1.0, 1.0, ALU.mult, ALU.add))
            for i in range(2):
                const(nc.vector.memset(v_own[i][:, :, :, HD:HD + 1], 1.0))
                const(nc.vector.memset(v_mix[i][:, :, :, HD:HD + 1], 1.0))
                const(nc.vector.memset(v_mix[i][0:WINDOW, 0, :, :], 0.0))
            for w, w_hi, w_lo in ((w_qk, w_qk_hi, w_qk_lo), (w_k, w_k_hi, w_k_lo)):
                const(nc.vector.tensor_copy(w_hi[:, :, :], w[:, :, :]))
                const(nc.vector.tensor_tensor(w_lo[:, :, :], w[:, :, :], w_hi[:, :, :].bitcast(FP32),
                                              ALU.subtract))
            const(nc.vector.tensor_scalar(w_f[:, :, :], w_f[:, :, :], 0.5, None, ALU.mult))
            const(nc.vector.tensor_copy(kact[:, :, 0:P], bv_col[:, :].rearrange("p (k o) -> p k o", o=1)
                                        .broadcast_to([P, KT, P])))
            nc.vector.memset(x2T[:, :, 0:1], 0.0).then_inc(dve_consts, 1)
            dve.wait_ge(dve_consts, 1)
            dve.wait_ge(bo_done, 1)
            nc.vector.tensor_copy(bo_all[:, :], bank_p[0][:, 0:D]).then_inc(bo_ready, 1)

            def aggregate(st, mv, s, stats, mv_ready):
                for t in range(TILES):
                    count = held(dve, s.after(TILES, t + 1))
                    dve.wait_ge(dve_consts, 1)
                    dve.wait_ge(stats, count)
                    nc.vector.bn_aggr(mv[:, t, :], st[:, t, :]).then_inc(mv_ready, 1)

            def normalise(xn, src, mv, rstd, ready):
                for t in range(TILES):
                    nc.vector.tensor_scalar(xn[:, t, :], src[:, t, :], mv[:, t, 0:1], rstd[:, t:t + 1],
                                            ALU.subtract, ALU.mult).then_inc(ready, 1)

            def clip(f, t):
                dve.wait_ge(qk_done, f.after(TILES, t + 1))
                if t == 0:
                    if past(count := f.after(TILES, 0)):
                        dve.wait_ge(qkT_done, count)
                nc.vector.tensor_scalar(qk[:, t, :], bank_p[0][:, :], -CLIP, CLIP, ALU.max, ALU.min)\
                    .then_inc(qk_clipped, 1)

            def sum_squares(f, t):
                dve.wait_ge(sq_ready, f.after(TILES, t + 1))
                if t == 0:
                    if past(count := f.after(1, 0)):
                        dve.wait_ge(rms_ready, count)
                nc.vector.tensor_reduce(rms_v[:, 2 * HEADS * t:2 * HEADS * (t + 1)].rearrange("p (g h) -> p g h", h=GROUP),
                                        sq[t % 2][:, :].rearrange("p (g r h) -> p g h r", r=HD, h=GROUP),
                                        AX.X, ALU.add).then_inc(sumsq_ready, 1)

            def maximum(s, n):
                t, c = n // 4, n % 4
                dve.wait_ge(a_done, s.after(BANKS, n + 1))
                if n == 0:
                    if past(count := s.after(1, 0)):
                        dve.wait_ge(maxT_done, count)
                nc.vector.tensor_reduce(smax[:, t, 4 * c:4 * c + 4],
                                        bank_a[n % 4][:, :].rearrange("p (h k) -> p h k", h=4),
                                        AX.X, ALU.max).then_inc(max_ready, 1)

            def attended(s, t):
                dve.wait_ge(pv_done, s.after(BANKS, 4 * t + 4))
                if past(count := s.after(2 * TILES, 2 * t)):
                    dve.wait_ge(o_normed, count)
                nc.vector.transpose(o_tok[:, :, :].rearrange("p c r -> p (c r)"), bank_o[t % 2][:, :])\
                    .then_inc(o_turned, 1)
                dve.wait_ge(o_turned, s.after(TILES, t + 1))
                nc.vector.reciprocal(o_inv[:, :], o_tok[:, :, HD]).then_inc(o_inverse, 1)
                dve.wait_ge(o_inverse, s.after(TILES, t + 1))
                if past(count := s.after(TILES, t)):
                    dve.wait_ge(oT_ready, count)
                tok = o_tok[:, :, :].rearrange("p (k o b) r -> p k o b r", k=KT, o=2)
                inv = o_inv[:, :].rearrange("p (k o b x) -> p k o b x", k=KT, o=2, x=1)
                for odd in range(2):
                    nc.vector.tensor_tensor(
                        o_nrm[:, :, :, HD * odd:HD * odd + HD], tok[:, :, odd, :, 0:HD],
                        inv[:, :, odd, :, :].broadcast_to([P, KT, 4, HD]), ALU.mult).then_inc(o_normed, 1)
                dve.wait_ge(o_normed, s.after(2 * TILES, 2 * t + 2))
                if t == 0:
                    if past(count := s.after(TILES, 0)):
                        dve.wait_ge(wo_done, count)
                nc.vector.transpose(oT[:, t, :, :].rearrange("p b n -> p (b n)"),
                                    o_nrm[:, :, :, :].rearrange("p k b r -> p (k b r)")).then_inc(oT_ready, 1)

            def residual(s, t, bank):
                dve.wait_ge(wo_done, s.after(TILES, t + 1))
                if t == 0:
                    dve.wait_ge(res_biased, s.after(1, 1))
                xt = x1[s.parity][:, t, :]
                nc.vector.tensor_tensor(xt, xt, bank[:, 0:D], ALU.add).then_inc(x1_ready, 1)

            def residual_stats(s, t):
                dve.wait_ge(x1_ready, s.after(TILES, t + 1))
                if t == 0:
                    if past(count := s.after(TILES, 0)):
                        dve.wait_ge(ln2_mv, count)
                nc.vector.bn_stats(st2[:, t, :], x1[s.parity][:, t, :]).then_inc(ln2_stats, 1)

            def less_part_0(f, g, t, ffn):
                dve.wait_ge(part0_ready, f.after(TILES, t + 1))
                if past(count := f.after(TILES, t - 1)):
                    dve.wait_ge(part2_ready, count)
                if t == 0 and ffn:
                    dve.wait_ge(mixed, g.after(2 * KT, 2 * KT))
                b4 = bank_t[t % 2][:, :].rearrange("p (b n) -> p b n", b=4)
                cols = slice(P * t, P * t + P)
                nc.vector.scalar_tensor_tensor(rest[t % 2][:, 0:2, :], b4[:, 0:2, :], qk_scale[:, :],
                                               parts[:, 0:2, 0, cols], ALU.mult, ALU.subtract)
                nc.vector.tensor_tensor(rest[t % 2][:, 2:4, :], b4[:, 2:4, :], parts[:, 2:4, 0, cols],
                                        ALU.subtract).then_inc(rest_ready, 1)

            def gate_kv(g, t):
                dve.wait_ge(kv_done, g.after(TILES, t + 1))
                dve.wait_ge(gate_ready, g.after(TILES, t + 1))
                nc.vector.scalar_tensor_tensor(gate[:, t, :], gate[:, t, :], 1.0, kv_bank[t][:, 0:D],
                                               ALU.add, ALU.mult).then_inc(kvr_ready, 1)

            def high_xT(e, k):
                dve.wait_ge(xT_ready, e.after(KT, k + 1))
                if k == 0:
                    if past(count := e.after(TILES, 0)):
                        dve.wait_ge(qk_done, count)
                nc.vector.tensor_copy(xT_hi[:, k, :], xT[:, k, :]).then_inc(xT_hi_ready, 1)

            def high_xk(g, k):
                dve.wait_ge(mixed, g.after(2 * KT, k + 1))
                if k == 0:
                    if past(count := g.after(KT, 0)):
                        dve.wait_ge(k_done, count)
                nc.vector.tensor_copy(xk_hi[:, k, :], xk[:, k, :]).then_inc(xk_hi_ready, 1)

            def stats_1(e, t):
                if t == 0:
                    dve.wait_ge(x_loaded, e.after(16, 16))
                    if past(count := e.after(TILES, 0)):
                        dve.wait_ge(ln1_mv, count)
                for i in (t, t + 1):
                    nc.vector.bn_stats(st1[:, i, :], x_in[:, i, :]).then_inc(ln1_stats, 1)

            def rms_inverse(f):
                dve.wait_ge(sumsq_ready, f.after(TILES, TILES))
                nc.vector.tensor_scalar(rms_v[:, :], rms_v[:, :], 1.0 / HD, RMS_EPS, ALU.mult, ALU.max)\
                    .then_inc(rms_step, 1)
                dve.wait_ge(rms_step, f.after(RMS_STEPS, 1))
                nc.vector.tensor_scalar(rms_v[:, :], rms_v[:, :], RMS_EPS, 0.5, ALU.add, ALU.mult).then_inc(rms_step, 1)
                dve.wait_ge(rms_step, f.after(RMS_STEPS, 2))
                if past(count := f.after(TILES, 0)):
                    dve.wait_ge(qkn_ready, count)
                nc.vector.tensor_scalar(rms_r[:, :].bitcast(INT32), rms_v[:, :].bitcast(INT32),
                                        -0.5, float(SEED), ALU.mult, ALU.add).then_inc(rms_step, 1)
                for i in range(NEWTON):
                    dve.wait_ge(rms_step, f.after(RMS_STEPS, 3 + 3 * i))
                    nc.vector.tensor_tensor(rms_w[:, :], rms_r[:, :], rms_r[:, :], ALU.mult).then_inc(rms_step, 1)
                    dve.wait_ge(rms_step, f.after(RMS_STEPS, 4 + 3 * i))
                    nc.vector.scalar_tensor_tensor(rms_w[:, :], rms_w[:, :], -1.0, rms_v[:, :], ALU.mult, ALU.mult)\
                        .then_inc(rms_step, 1)
                    dve.wait_ge(rms_step, f.after(RMS_STEPS, 5 + 3 * i))
                    nc.vector.scalar_tensor_tensor(rms_r[:, :], rms_w[:, :], 1.5, rms_r[:, :], ALU.add, ALU.mult)\
                        .then_inc(rms_ready if i == NEWTON - 1 else rms_step, 1)

            def body(s, lead, front, attend, ffn):
                e, f, g = s.shifted(2), s.shifted(1), s.shifted(-1)
                if ffn:
                    dve.wait_ge(ln2_rstd, g.after(1, 1))
                    if past(count := g.after(TILES, 0)):
                        dve.wait_ge(kv_done, count)
                    normalise(xn2, x1[g.parity], mv2, rstd2, xn2_ready)
                if front:
                    clip(f, 0)
                for n in range(BANKS):
                    if attend:
                        maximum(s, n)
                    if front and n in QK_AT:
                        sum_squares(f, QK_AT.index(n))
                        clip(f, QK_AT.index(n) + 1)
                    if lead and n in V_AT:
                        stats_1(e, 2 * V_AT.index(n))
                    if ffn and n in (9, 12):
                        high_xk(g, (9, 12).index(n))
                if lead:
                    aggregate(st1, mv1, e, ln1_stats, ln1_mv)
                if front:
                    sum_squares(f, TILES - 2)
                    clip(f, TILES - 1)
                if attend:
                    dve.wait_ge(maxT_done, s.after(1, 1))
                    dve.wait_ge(neg0_ready, s.after(1, 1))
                    if past(count := s.after(1, 0)):
                        dve.wait_ge(neg2_ready, count)
                    nc.vector.scalar_tensor_tensor(neg_rest[:, :], bank_s[0][0:HEADS, :], -1.0, neg_p[0][:, :],
                                                   ALU.mult, ALU.subtract).then_inc(neg_rest_ready, 1)
                if front:
                    sum_squares(f, TILES - 1)
                if attend:
                    dve.wait_ge(neg_rest_ready, s.after(1, 1))
                    dve.wait_ge(neg1_ready, s.after(1, 1))
                    if past(count := s.after(16 * PARTS, 0)):
                        dve.wait_ge(max_rows_loaded, count)
                    nc.vector.tensor_tensor(neg_p[2][:, :], neg_rest[:, :], neg_p[1][:, :], ALU.subtract)\
                        .then_inc(neg2_ready, 1)
                if front:
                    rms_inverse(f)
                if front:
                    for t in range(TILES):
                        if t == 0:
                            dve.wait_ge(rms_ready, f.after(1, 1))
                            dve.wait_ge(sq_ready, f.after(TILES, TILES))
                        q4 = qk[:, t, :].rearrange("p (g r h) -> p g r h", r=HD, h=GROUP)
                        r4 = rms_r[:, 2 * HEADS * t:2 * HEADS * (t + 1)].rearrange("p (g x h) -> p g x h", x=1, h=GROUP)
                        nc.vector.tensor_tensor(q4, q4, r4.broadcast_to([P, 2 * KT, HD, GROUP]), ALU.mult)\
                            .then_inc(qkn_ready, 1)
                for n in range(BANKS):
                    t = n // 4
                    if front and n in SPLIT_AT:
                        less_part_0(f, g, SPLIT_AT.index(n), ffn)
                    if attend and n % 4 == 3:
                        if t:
                            residual(s, t - 1, bank_p[(t - 1) % 2])
                            if t > 1:
                                residual_stats(s, t - 2)
                    if lead and n == BANKS - 1:
                        high_xT(e, 0)
                    if attend and n % 4 == 3:
                        attended(s, t)
                if ffn:
                    gate_kv(g, 0)
                if lead:
                    high_xT(e, 1)
                if ffn:
                    gate_kv(g, 1)
                if attend:
                    residual_stats(s, TILES - 2)
                    if past(count := s.after(1, 0)):
                        dve.wait_ge(ln2_rstd, count)
                    if past(count := s.after(TILES, 0)):
                        dve.wait_ge(xn2_ready, count)
                    residual(s, TILES - 1, bank_o[0])
                    residual_stats(s, TILES - 1)
                    aggregate(st2, mv2, s, ln2_stats, ln2_mv)
                if ffn:
                    gate_kv(g, 2)
                    gate_kv(g, 3)
                if front and not attend:
                    for i in range(2):
                        nc.vector.memset(k_st[i][STACK:ROWS, :, :].bitcast(INT32), ONES_PAIR)

            schedule(dve, body)

        @block.tensor
        def _(pe):
            pe.wait_ge(pool_consts, 1)
            pe.wait_ge(dve_consts, 1)
            pe.wait_ge(consts_loaded, 16 * CONSTS)

            def add_bias(dst, lo, n):
                nc.tensor.matmul(dst, ones_rows[:, :], bias_p[:, lo:lo + n], start=True, stop=False)

            def transposes(xn, k, done):
                for t in range(TILES):
                    last = nc.tensor.transpose(bank_t[k][:, P * t:P * t + P], xn[:, t, P * k:P * k + P],
                                               ident[:, :])
                last.then_inc(done, 1)

            def token_product(dst, lhs, w, first, done):
                for k in range(KT):
                    last = nc.tensor.matmul(dst, lhs(k), w[:, k, :], start=(first and k == 0), stop=(k == KT - 1))
                last.then_inc(done, 1)

            def project_qk(s, f, t):
                if past(count := f.after(TILES, t)):
                    pe.wait_ge(qk_clipped, count)
                if t == 0:
                    if past(count := s.after(TILES, 0)):
                        pe.wait_ge(x1_ready, count)
                    if past(count := s.after(TILES, -TILES - 2)):
                        pe.wait_ge(kvr_ready, count)
                    pe.wait_ge(xT_lo_ready, f.after(KT, KT))
                add_bias(bank_p[0][:, :], 0, 2 * D)
                for k in range(KT):
                    for x_half, w_half in ((xT_hi, w_qk_hi), (xT_hi, w_qk_lo), (xT_lo, w_qk_hi)):
                        last = nc.tensor.matmul(
                            bank_p[0][:, :], x_half[:, k, P * t:P * t + P], w_half[:, k, :], start=False,
                            stop=(k == KT - 1 and x_half is xT_lo))
                last.then_inc(qk_done, 1)

            def project_v(s, f, t):
                if past(count := f.after(TILES, t)):
                    pe.wait_ge(v_ready, count)
                if t == 0:
                    if past(count := s.after(TILES, -TILES)):
                        pe.wait_ge(kvr_ready, count)
                token_product(bank_p[1][:, 0:D], lambda k: xT[:, k, P * t:P * t + P], w_v, True, v_done)

            def scores_a(s, n):
                q, k = q_st[s.parity], k_st[s.parity]
                t, c = n // 4, n % 4
                dst = bank_a[n % 4]
                if n < 2:
                    if past(count := s.after(BANKS, 0)):
                        pe.wait_ge(prob_ready, count)
                elif n == 2:
                    if past(count := s.after(TILES, 0)):
                        pe.wait_ge(x1_ready, count)
                elif n == 3:
                    if past(count := s.after(TILES, 0)):
                        pe.wait_ge(o_turned, count)
                    if past(count := s.after(TILES, -TILES - 1)):
                        pe.wait_ge(kvr_ready, count)
                else:
                    pe.wait_ge(max_ready, s.after(BANKS, n - 3))
                nc.tensor.matmul(dst[:, :], ident_b[:, :],
                                 mask_a[min(t, 1)][:, :, :].rearrange("p h k -> p (h k)"),
                                 start=True, stop=False, skip_group_check=True)
                for j in range(4):
                    for half in range(2):
                        h, i = 4 * c + j, 2 * t + half
                        lo = max(0, WINDOW * (i - 1))
                        hi = WINDOW * (i + 1)
                        last = nc.tensor.matmul(
                            dst[WINDOW * half:WINDOW * half + WINDOW, P * (j + 1) - (hi - lo):P * (j + 1)],
                            q[0:STACK, h, WINDOW * i:hi], k[0:STACK, h, lo:hi],
                            start=False, stop=True, skip_group_check=True)
                last.then_inc(a_done, 1)

            def scores_b(s, n):
                q, k = q_st[s.parity], k_st[s.parity]
                i, c = n // 2, n % 2
                dst = bank_s[n % 2]
                if n < 2:
                    pe.wait_ge(max_ready, s.after(BANKS, BANKS))
                else:
                    pe.wait_ge(prob_ready, s.after(BANKS, n - 1))
                nc.tensor.matmul(dst[:, :], ident_b[:, :],
                                 mask_b[min(i, 1)][:, :, :].rearrange("p h q -> p (h q)"),
                                 start=True, stop=False, skip_group_check=True)
                for j in range(8):
                    h = 8 * c + j
                    lo, hi = max(0, WINDOW * (i - 1)), WINDOW * (i + 1)
                    last = nc.tensor.matmul(dst[P - (hi - lo):P, WINDOW * j:WINDOW * j + WINDOW],
                                            k[0:ROWS, h, lo:hi], q[0:ROWS, h, WINDOW * i:hi],
                                            start=False, stop=True, skip_group_check=True)
                last.then_inc(b_done, 1)

            def times_v(s, g, n, ffn):
                i, c = n // 2, n % 2
                t = i // 2
                v = v_own[s.parity] if i % 2 else v_mix[s.parity]
                pe.wait_ge(prob_ready, s.after(BANKS, n + 1))
                if n % 4 == 0:
                    if t < 2 and ffn:
                        pe.wait_ge(gate_ready, g.after(TILES, t + 3))
                    if past(count := s.after(TILES, t - 1)):
                        pe.wait_ge(o_turned, count)
                for j in range(8):
                    h = 8 * c + j
                    quad, row = h // 4, 32 * (h % 4)
                    col = P * quad + WINDOW * (i % 2)
                    last = nc.tensor.matmul(bank_o[t % 2][row:row + HD + 1, col:col + WINDOW],
                                            v[:, t, h, :], prob[n % 3][:, j, :], start=True, stop=True,
                                            tile_position=(0, row))
                last.then_inc(pv_done, 1)

            def output_product(s, t, bank):
                pe.wait_ge(oT_ready, s.after(TILES, t + 1))
                token_product(bank[:, 0:D], lambda k: oT[:, t, k, :], w_o, True, wo_done)

            def transpose_qk(f, t):
                pe.wait_ge(qkn_ready, f.after(TILES, t + 1))
                if t >= 2:
                    pe.wait_ge(part0_ready, f.after(TILES, t - 1))
                    pe.wait_ge(rest_ready, f.after(TILES, t - 1))
                for b in range(2 * KT):
                    last = nc.tensor.transpose(bank_t[t % 2][:, P * b:P * b + P], qk[:, t, P * b:P * b + P],
                                               ident[:, :])
                last.then_inc(qkT_done, 1)

            def ffn_k(g, m):
                for k in range(KT):
                    for i, (w_half, x_half) in enumerate(((w_k_hi, xk_hi), (w_k_lo, xk_hi), (w_k_hi, xk_lo))):
                        last = nc.tensor.matmul(
                            bank_t[m][:, :], w_half[:, k, P * m:P * m + P], x_half[:, k, :], start=(k == 0 and i == 0),
                            stop=(k == KT - 1 and i == 2))
                last.then_inc(k_done, 1)

            def ffn_r(s, f, g, t, front, attend):
                if t < 2 and front:
                    pe.wait_ge(qk_clipped, f.after(TILES, TILES))
                    pe.wait_ge(v_ready, f.after(TILES, TILES))
                elif t >= 2 and attend:
                    pe.wait_ge(max_ready, s.after(BANKS, BANKS))
                else:
                    pe.wait_ge(x1_ready, g.after(TILES, TILES))
                    pe.wait_ge(kvr_ready, g.after(TILES, 0))
                token_product(r_bank[t][:, 0:D], lambda k: xr[:, k, P * t:P * t + P], w_r, True, r_done)

            def ffn_kv(g, t):
                token_product(kv_bank[t][:, 0:D], lambda k: kact[:, k, P * t:P * t + P], w_f, True, kv_done)

            def body(s, lead, front, attend, ffn):
                e, f, g = s.shifted(2), s.shifted(1), s.shifted(-1)
                if front:
                    project_qk(s, f, 0)
                    project_v(s, f, 0)
                for n in range(BANKS):
                    if attend:
                        if n == 0:
                            pe.wait_ge(stack_loaded[s.parity], s.after_half(STACK_LOADS, STACK_LOADS))
                        scores_a(s, n)
                    if ffn and n == 1:
                        pe.wait_ge(xn2_ready, g.after(TILES, TILES))
                        if front:
                            pe.wait_ge(xT_ready, f.after(KT, KT))
                        else:
                            pe.wait_ge(relu_ready, g.after(KT, 0))
                            if attend:
                                pe.wait_ge(part0_ready, s.after(TILES, TILES))
                                pe.wait_ge(rest_ready, s.after(TILES, TILES))
                        for k in range(KT):
                            transposes(xn2, k, x2T_done)
                    if front and n in QK_AT:
                        project_qk(s, f, QK_AT.index(n) + 1)
                    if front and n in V_AT:
                        project_v(s, f, V_AT.index(n) + 1)
                if front:
                    project_qk(s, f, TILES - 1)
                if attend:
                    pe.wait_ge(max_ready, s.after(BANKS, BANKS))
                    for t in range(TILES):
                        last = nc.tensor.transpose(bank_s[0][0:HEADS, P * t:P * t + P], smax[:, t, :], ident[:, :])
                    last.then_inc(maxT_done, 1)
                if front:
                    project_v(s, f, TILES - 1)
                if ffn:
                    pe.wait_ge(xk_lo_ready, g.after(KT, KT))
                    pe.wait_ge(x2T_ready, g.after(KT, KT))
                    ffn_k(g, 0)
                    ffn_k(g, 1)
                    for t in range(TILES - 1):
                        ffn_r(s, f, g, t, front, attend)
                if attend:
                    pe.wait_ge(max_rows_loaded, s.after(16 * PARTS, 16 * PARTS))
                    scores_b(s, 0)
                if ffn:
                    ffn_r(s, f, g, TILES - 1, front, attend)
                if front:
                    if ffn:
                        pe.wait_ge(relu_ready, g.after(KT, KT))
                    pe.wait_ge(xT_ready, f.after(KT, KT))
                for n in range(BANKS):
                    if attend and n + 1 < BANKS:
                        scores_b(s, n + 1)
                    if front and n + 1 in SPLIT_AT:
                        transpose_qk(f, SPLIT_AT.index(n + 1))
                    if lead and n == BANKS - 1:
                        pe.wait_ge(xn1_ready, e.after(TILES, TILES))
                        if past(count := e.after(TILES, 0)):
                            pe.wait_ge(part0_ready, count)
                            pe.wait_ge(rest_ready, count)
                        transposes(x_in, 0, xT_done)
                    if attend and n % 4 == 3 and n > 4:
                        t = n // 4 - 1
                        if t < 2 and ffn:
                            pe.wait_ge(gate_ready, g.after(TILES, TILES))
                        elif t < 2 and front:
                            pe.wait_ge(qk_clipped, f.after(TILES, TILES))
                            pe.wait_ge(v_ready, f.after(TILES, TILES))
                        if t == 2:
                            pe.wait_ge(x1_ready, s.after(TILES, 1))
                        output_product(s, t, bank_p[t % 2])
                    if attend:
                        times_v(s, g, n, ffn)
                if ffn:
                    pe.wait_ge(kact_ready, g.after(KT, KT))
                    for t in range(2):
                        if attend:
                            pe.wait_ge(x1_ready, s.after(TILES, t + 2))
                        else:
                            pe.wait_ge(gate_ready, g.after(TILES, TILES))
                        ffn_kv(g, t)
                        if t == 0 and lead:
                            transposes(x_in, 1, xT_done)
                    pe.wait_ge(o_turned, (s if attend else g).after(TILES, TILES))
                    ffn_kv(g, 2)
                elif lead:
                    transposes(x_in, 1, xT_done)
                if attend:
                    pe.wait_ge(o_turned, s.after(TILES, TILES - 1))
                    output_product(s, TILES - 1, bank_o[0])
                if ffn:
                    pe.wait_ge(kvr_ready, g.after(TILES, 1))
                    ffn_kv(g, 3)

            add_bias(bank_p[0][:, 0:D], 2 * D, D)
            token_product(bank_p[0][:, 0:D], lambda k: kact[:, k, 0:P], w_o, False, bo_done)
            pe.wait_ge(bo_ready, 1)
            schedule(pe, body)


def kernel(L0_attn_x, L0_attn_wq_w, L0_attn_wq_b, L0_attn_wk_w, L0_attn_wk_b, L0_attn_wv_w, L0_attn_wv_b,
           L0_attn_wo_w, L0_attn_wo_b, L0_attn_qn_w, L0_attn_kn_w, L0_ffn_W_r, L0_ffn_W_k, L0_ffn_W_v,
           L0_ffn_mu_r, L0_ffn_mu_k):
    import concourse.bacc as bacc
    from concourse.bass_utils import run_bass_kernel_spmd

    def by_group(w):
        return np.asarray(w).reshape(GROUP, KT, HD, -1).transpose(1, 2, 0, 3).reshape(D, -1)

    wo = np.asarray(L0_attn_wo_w).T.reshape(KT, 2, 4, HD, D).transpose(0, 2, 1, 3, 4)
    arrays = {
        "x": np.asarray(L0_attn_x).reshape(SEQS * L, D),
        "wqkT": np.concatenate([by_group(L0_attn_wq_w).T, by_group(L0_attn_wk_w).T], axis=1),
        "wvT": np.asarray(L0_attn_wv_w).T,
        "woP": wo.reshape(D, D),
        "wrT": np.asarray(L0_ffn_W_r).T,
        "wkT": np.asarray(L0_ffn_W_k).T,
        "wfT": np.asarray(L0_ffn_W_v).T,
        "bqk": np.concatenate([by_group(L0_attn_wq_b), by_group(L0_attn_wk_b)]).reshape(1, 2 * D),
        "bo": np.asarray(L0_attn_wo_b).reshape(1, D),
        "bv": np.asarray(L0_attn_wv_b).reshape(KT, 2, 4, HD).transpose(0, 2, 1, 3).reshape(KT, P).T,
        "qn": np.repeat(np.asarray(L0_attn_qn_w), GROUP).reshape(P, 1),
        "kn": np.repeat(np.asarray(L0_attn_kn_w), GROUP).reshape(P, 1),
        "mu": np.stack([np.asarray(L0_ffn_mu_r).reshape(KT, P), np.asarray(L0_ffn_mu_k).reshape(KT, P)])
        .transpose(2, 0, 1),
    }
    arrays = {k: np.ascontiguousarray(v) for k, v in arrays.items()}
    nc = bacc.Bacc("TRN2", target_bir_lowering=False, num_devices=1)
    ins = [nc.dram_tensor(k, v.shape, FP32, kind="ExternalInput").ap() for k, v in arrays.items()]
    out = nc.dram_tensor("out", (SEQS * L, D), FP32, kind="ExternalOutput").ap()
    build(nc, *ins, out)
    r = run_bass_kernel_spmd(nc, [arrays], core_ids=[0])
    return r.results[0]["out"].reshape(SEQS, L, D)
```
